# Optimizing a Trainium2 kernel written in Bass

```python
import numpy as np
import jax
import jax.numpy as jnp

def _softmax(x, axis=-1):
    return jax.nn.softmax(x, axis=axis)

def _gelu(x):
    return jax.nn.gelu(x, approximate=True)

def _silu(x):
    return jax.nn.silu(x)

def _sigmoid(x):
    return jax.nn.sigmoid(x)

def _layernorm(x, axis=-1, eps=1e-05):
    m = jnp.mean(x, axis=axis, keepdims=True)
    v = jnp.var(x, axis=axis, keepdims=True)
    return (x - m) / jnp.sqrt(v + eps)

def _scatter_add(tgt, idx, src, axis=0):
    return tgt.at[idx].add(src)

def _segment_sum(src, seg, n):
    return jax.ops.segment_sum(src, seg, n)
kernel_name = 'mk_decoder_postln_d1_seqx_r4_6bf86f'

def setup_inputs(seed: int=0):
    np.random.seed(seed)
    _w = jnp.asarray

    def _rec_inputs():
        import jax
        import jax.numpy as jnp
        _rk = jax.random.key(seed)
        x = 7.22e-05 + 1 * jax.random.normal(jax.random.fold_in(_rk, 1), (16, 100, 512), jnp.float32)
        _lenS = 100 - jax.random.randint(jax.random.fold_in(_rk, 7), (16,), 0, max(1, 100 // 4) + 1, jnp.int32)
        _lenS2 = 361 - jax.random.randint(jax.random.fold_in(_rk, 8), (16,), 0, max(1, 361 // 4) + 1, jnp.int32)
        _ctx_512P = jax.random.normal(jax.random.fold_in(_rk, 11), (16, 16, 128), jnp.float32)
        _ctx_512c = jax.random.dirichlet(jax.random.fold_in(_rk, 511), 0.3 * jnp.ones((16,), jnp.float32), (16, 361))
        _ctx_512t = jnp.einsum('bsk,bkd->bsd', _ctx_512c, _ctx_512P)
        _ctx_512t = _ctx_512t * jax.lax.rsqrt(jnp.mean(jnp.square(_ctx_512t)) + 1e-12) * 0.953939
        ctx_512 = -0.000514642 + 1.00011 * (_ctx_512t + 0.3 * jax.random.normal(jax.random.fold_in(_rk, 611), (16, 361, 128), jnp.float32))
        return (x, ctx_512)
    x, ctx_512 = _rec_inputs()

    def _L0_attn_setup():
        import jax, jax.numpy as jnp
        import numpy as np
        B, T, D = (2, 512, 512)
        HQ, HKV = (32, 8)
        HD = D // HQ
        G = HQ // HKV
        ROPE_BASE = 10000.0

        def _rope(q, k):
            t, d = (q.shape[2], q.shape[3])
            inv_freq = 1.0 / ROPE_BASE ** (jnp.arange(0, d, 2, dtype=jnp.float32) / d)
            ang = jnp.arange(t, dtype=jnp.float32)[:, None] * inv_freq[None, :]
            cos = jnp.concatenate([jnp.cos(ang), jnp.cos(ang)], axis=-1)[None, None]
            sin = jnp.concatenate([jnp.sin(ang), jnp.sin(ang)], axis=-1)[None, None]

            def rot_half(x):
                x1, x2 = jnp.split(x, 2, axis=-1)
                return jnp.concatenate([-x2, x1], axis=-1)
            return (q * cos + rot_half(q) * sin, k * cos + rot_half(k) * sin)
        key = jax.random.key(seed)
        ks = jax.random.split(key, 5)
        s = 0.02
        x = jax.random.normal(ks[0], (B, T, D), dtype=jnp.float32)
        Wq = jax.random.normal(ks[1], (D, D), dtype=jnp.float32) * s
        Wk = jax.random.normal(ks[2], (HKV * HD, D), dtype=jnp.float32) * s
        Wv = jax.random.normal(ks[3], (HKV * HD, D), dtype=jnp.float32) * s
        Wo = jax.random.normal(ks[4], (D, D), dtype=jnp.float32) * s
        return {'x': x, 'Wq': Wq, 'bq': jnp.zeros((D,), jnp.float32), 'Wk': Wk, 'bk': jnp.zeros((HKV * HD,), jnp.float32), 'Wv': Wv, 'bv': jnp.zeros((HKV * HD,), jnp.float32), 'Wo': Wo, 'bo': jnp.zeros((D,), jnp.float32)}
    _L0_attn_all = _L0_attn_setup()
    _L0_attn_in = {k: v for k, v in _L0_attn_all.items() if k in ('Wq', 'bq', 'Wk', 'bk', 'Wv', 'bv', 'Wo', 'bo')}
    del _L0_attn_all

    def _L0_xattn_setup():
        import jax, jax.numpy as jnp
        import numpy as np
        B, S, H, NH, L = (2, 512, 512, 16, 128)
        HD = H // NH
        key = jax.random.key(seed)
        k1, k2, k3, k4, k5 = jax.random.split(key, 5)
        scale = 0.02
        return {'q': jax.random.normal(k1, (B, S, H), dtype=jnp.float32), 'latent_kv': jax.random.normal(k2, (B, S, L), dtype=jnp.float32), 'Wq': jax.random.normal(k3, (H, H), dtype=jnp.float32) * scale, 'Wkv_expand': jax.random.normal(k4, (2 * H, L), dtype=jnp.float32) * scale, 'Wout': jax.random.normal(k5, (H, H), dtype=jnp.float32) * scale}
    _L0_xattn_all = _L0_xattn_setup()
    _L0_xattn_in = {k: v for k, v in _L0_xattn_all.items() if k in ('Wq', 'Wkv_expand', 'Wout')}
    del _L0_xattn_all

    def _L0_ffn_setup():
        import jax, jax.numpy as jnp
        import numpy as np
        B, S, D, E, TOPK = (4, 512, 512, 8, 2)
        key = jax.random.key(seed)
        k1, k2, k3 = jax.random.split(key, 3)
        x = jax.random.normal(k1, (B, S, D), dtype=jnp.float32)
        gate_w = jax.random.normal(k2, (E, D), dtype=jnp.float32) * 0.02
        expert_w = jax.random.normal(k3, (E, D, D), dtype=jnp.float32) / np.sqrt(D)
        expert_b = jnp.zeros((E, D), dtype=jnp.float32)
        return {'x': x, 'gate_w': gate_w, 'expert_w': expert_w, 'expert_b': expert_b}
    _L0_ffn_all = _L0_ffn_setup()
    _L0_ffn_in = {k: v for k, v in _L0_ffn_all.items() if k in ('gate_w', 'expert_w', 'expert_b')}
    del _L0_ffn_all
    return {'x': x, 'ctx_512': ctx_512, 'L0_attn_Wq': _L0_attn_in['Wq'], 'L0_attn_bq': _L0_attn_in['bq'], 'L0_attn_Wk': _L0_attn_in['Wk'], 'L0_attn_bk': _L0_attn_in['bk'], 'L0_attn_Wv': _L0_attn_in['Wv'], 'L0_attn_bv': _L0_attn_in['bv'], 'L0_attn_Wo': _L0_attn_in['Wo'], 'L0_attn_bo': _L0_attn_in['bo'], 'L0_xattn_Wq': _L0_xattn_in['Wq'], 'L0_xattn_Wkv_expand': _L0_xattn_in['Wkv_expand'], 'L0_xattn_Wout': _L0_xattn_in['Wout'], 'L0_ffn_gate_w': _L0_ffn_in['gate_w'], 'L0_ffn_expert_w': _L0_ffn_in['expert_w'], 'L0_ffn_expert_b': _L0_ffn_in['expert_b']}

def reference(x, ctx_512, L0_attn_Wq, L0_attn_bq, L0_attn_Wk, L0_attn_bk, L0_attn_Wv, L0_attn_bv, L0_attn_Wo, L0_attn_bo, L0_xattn_Wq, L0_xattn_Wkv_expand, L0_xattn_Wout, L0_ffn_gate_w, L0_ffn_expert_w, L0_ffn_expert_b):
    import jax
    import jax.numpy as jnp

    def _L0_attn_ref(x, Wq, bq, Wk, bk, Wv, bv, Wo, bo):
        import jax, jax.numpy as jnp
        import numpy as np
        B, T, D = (2, 512, 512)
        HQ, HKV = (32, 8)
        HD = D // HQ
        G = HQ // HKV
        ROPE_BASE = 10000.0

        def _rope(q, k):
            t, d = (q.shape[2], q.shape[3])
            inv_freq = 1.0 / ROPE_BASE ** (jnp.arange(0, d, 2, dtype=jnp.float32) / d)
            ang = jnp.arange(t, dtype=jnp.float32)[:, None] * inv_freq[None, :]
            cos = jnp.concatenate([jnp.cos(ang), jnp.cos(ang)], axis=-1)[None, None]
            sin = jnp.concatenate([jnp.sin(ang), jnp.sin(ang)], axis=-1)[None, None]

            def rot_half(x):
                x1, x2 = jnp.split(x, 2, axis=-1)
                return jnp.concatenate([-x2, x1], axis=-1)
            return (q * cos + rot_half(q) * sin, k * cos + rot_half(k) * sin)
        b, t, _ = x.shape
        Q = (x @ Wq.T + bq).reshape(b, t, HQ, HD).transpose(0, 2, 1, 3)
        K = (x @ Wk.T + bk).reshape(b, t, HKV, HD).transpose(0, 2, 1, 3)
        V = (x @ Wv.T + bv).reshape(b, t, HKV, HD).transpose(0, 2, 1, 3)
        Q, K = _rope(Q, K)
        K = jnp.repeat(K, G, axis=1)
        V = jnp.repeat(V, G, axis=1)
        scores = jnp.einsum('bhqd,bhkd->bhqk', Q, K) / np.sqrt(HD).astype(np.float32)
        w = jax.nn.softmax(scores, axis=-1)
        attn = jnp.einsum('bhqk,bhkd->bhqd', w, V)
        out = attn.transpose(0, 2, 1, 3).reshape(b, t, D)
        return out @ Wo.T + bo

    def _L0_xattn_ref(q, latent_kv, Wq, Wkv_expand, Wout):
        import jax, jax.numpy as jnp
        import numpy as np
        B, S, H, NH, L = (2, 512, 512, 16, 128)
        HD = H // NH
        b, sq, _ = q.shape
        sk = latent_kv.shape[1]
        qp = q @ Wq.T
        kv = latent_kv @ Wkv_expand.T
        k, v = jnp.split(kv, 2, axis=-1)
        qh = qp.reshape(b, sq, NH, HD).transpose(0, 2, 1, 3)
        kh = k.reshape(b, sk, NH, HD).transpose(0, 2, 1, 3)
        vh = v.reshape(b, sk, NH, HD).transpose(0, 2, 1, 3)
        inv_sqrt_d = 1.0 / jnp.sqrt(jnp.float32(HD))
        scores = jnp.einsum('bhqd,bhkd->bhqk', qh, kh) * inv_sqrt_d
        causal = jnp.tril(jnp.ones((sq, sk), dtype=bool))
        scores = jnp.where(causal, scores, jnp.finfo(scores.dtype).min)
        attn = jax.nn.softmax(scores, axis=-1)
        out = jnp.einsum('bhqk,bhkd->bhqd', attn, vh)
        out = out.transpose(0, 2, 1, 3).reshape(b, sq, H)
        return out @ Wout.T

    def _L0_ffn_ref(x, gate_w, expert_w, expert_b):
        import jax, jax.numpy as jnp
        import numpy as np
        B, S, D, E, TOPK = (4, 512, 512, 8, 2)
        batch_shape = x.shape[:-1]
        xf = x.reshape(-1, x.shape[-1])
        T = xf.shape[0]
        logits = jnp.einsum('td,ed->te', xf, gate_w)
        top_w, top_i = jax.lax.top_k(logits, TOPK)
        top_w = jax.nn.softmax(top_w.astype(jnp.float32), axis=-1).astype(x.dtype)
        gates = jnp.zeros((T, logits.shape[-1]), dtype=x.dtype)
        gates = gates.at[jnp.arange(T)[:, None], top_i].set(top_w)
        y = jnp.einsum('td,edo->eto', xf, expert_w) + expert_b[:, None, :]
        out = jnp.einsum('te,eto->to', gates, y)
        return out.reshape(*batch_shape, -1)
    x = _layernorm(x + _L0_attn_ref(x, L0_attn_Wq, L0_attn_bq, L0_attn_Wk, L0_attn_bk, L0_attn_Wv, L0_attn_bv, L0_attn_Wo, L0_attn_bo), axis=-1)
    x = _layernorm(x + _L0_xattn_ref(x, ctx_512, L0_xattn_Wq, L0_xattn_Wkv_expand, L0_xattn_Wout), axis=-1)
    x = _layernorm(x + _L0_ffn_ref(x, L0_ffn_gate_w, L0_ffn_expert_w, L0_ffn_expert_b), axis=-1)
    return x

_drawn_inputs = setup_inputs


def setup_inputs(seed=0):
    import zlib

    import numpy as np

    out = dict(_drawn_inputs(seed))
    spreads = {'L0_attn_bq': (0.0, 1.388),
     'L0_attn_bk': (0.0, 0.303),
     'L0_attn_bv': (0.0, 0.1),
     'L0_attn_bo': (0.0, 0.1),
     'L0_ffn_expert_b': (0.0, 0.1)}
    factors = {'L0_xattn_Wq': 2.87}
    for name, (base, spread) in spreads.items():
        noise = np.random.default_rng([zlib.crc32(name.encode()), seed]).standard_normal(out[name].shape)
        drawn = base * np.exp(spread * noise) if base else spread * noise
        out[name] = jnp.asarray(drawn.astype(out[name].dtype))
    for name, factor in factors.items():
        out[name] = (out[name] * factor).astype(out[name].dtype)
    return out
```

```python
from contextlib import ExitStack

import concourse.bass as bass
from concourse import mybir

F32 = mybir.dt.float32
F32R = mybir.dt.float32r
U32 = mybir.dt.uint32
ALU = mybir.AluOpType
ACT = mybir.ActivationFunctionType
AX_X = mybir.AxisListType.X

B, T, D, P = 16, 100, 512, 128
KC = D // P
HQ, HKV, HD = 32, 8, 16
J = HQ // HKV
XH, XD = 16, 32
XC = 4
KVW = HKV * HD
QKW = D + KVW
QKVW = D + 2 * KVW
E = 8
EPS = 1e-5
SELF_SCALE = HD ** -0.5
CROSS_SCALE = XD ** -0.5
YB = 4


def build_decoder(nc, x, xT, ctxT, w_qkv, b_qkv, w_o, b_o, w_xkv, w_xq, w_xo, w_gate, w_exp, b_exp,
                  rope_cos, rope_sin, ident_c, select_c, causal_c, prob_cap_c, expert_ids_c, out):
    with ExitStack() as ctx:
        def sb(name, shape, dt=F32, stack=ctx):
            return stack.enter_context(nc.sbuf_tensor(name, shape, dt))

        def sem(name):
            return ctx.enter_context(nc.semaphore(name))

        const_loaded = sem("const_loaded")
        const_ready = sem("const_ready")
        w_high = sem("w_high")
        w_ready = sem("w_ready")
        xT_loaded = sem("xT_loaded")
        xin_loaded = sem("xin_loaded")
        x_high = sem("x_high")
        x_split = sem("x_split")
        ctx_loaded = sem("ctx_loaded")
        c_high = sem("c_high")
        c_split = sem("c_split")
        xres_ready = sem("xres_ready")
        q_done = sem("q_done")
        kv_done = sem("kv_done")
        q_ready = sem("q_ready")
        k_ready = sem("k_ready")
        kv_ready = sem("kv_ready")
        roped_cos = sem("roped_cos")
        roped_sin = sem("roped_sin")
        roped = sem("roped")
        qk_high = sem("qk_high")
        qk_split = sem("qk_split")
        tqk_done = sem("tqk_done")
        tqk_read = sem("tqk_read")
        s_done = sem("s_done")
        s_max = sem("s_max")
        mt_done = sem("mt_done")
        mt_read = sem("mt_read")
        st_done = sem("st_done")
        exp_done = sem("exp_done")
        pv_done = sem("pv_done")
        recip_done = sem("recip_done")
        self_norm = sem("self_norm")
        ot_done = sem("ot_done")
        ot_high = sem("ot_high")
        ot_split = sem("ot_split")
        wo_done = sem("wo_done")
        res_added = sem("res_added")
        stats_done = sem("stats_done")
        mom_done = sem("mom_done")
        eps_done = sem("eps_done")
        rstd_done = sem("rstd_done")
        x1_ready = sem("x1_ready")
        x1t_done = sem("x1t_done")
        x1t_high = sem("x1t_high")
        x1t_split = sem("x1t_split")
        x1_kept = sem("x1_kept")
        xk_done = sem("xk_done")
        xk_copied = sem("xk_copied")
        xq_done = sem("xq_done")
        xq_copied = sem("xq_copied")
        xv_done = sem("xv_done")
        xv_copied = sem("xv_copied")
        xqt_done = sem("xqt_done")
        xqt_high = sem("xqt_high")
        xqt_split = sem("xqt_split")
        xkt_done = sem("xkt_done")
        xkt_high = sem("xkt_high")
        xkt_split = sem("xkt_split")
        sx_done = sem("sx_done")
        sx_masked = sem("sx_masked")
        sx_max = sem("sx_max")
        mxt_done = sem("mxt_done")
        mxt_read = sem("mxt_read")
        stx_done = sem("stx_done")
        expx_done = sem("expx_done")
        px_masked = sem("px_masked")
        pvx_done = sem("pvx_done")
        xrecip_done = sem("xrecip_done")
        cross_norm = sem("cross_norm")
        oxt_done = sem("oxt_done")
        oxt_high = sem("oxt_high")
        oxt_split = sem("oxt_split")
        wxo_done = sem("wxo_done")
        yres_added = sem("yres_added")
        ystats_done = sem("ystats_done")
        ymom_done = sem("ymom_done")
        yeps_done = sem("yeps_done")
        yrstd_done = sem("yrstd_done")
        x2_ready = sem("x2_ready")
        moe_loaded = sem("moe_loaded")
        moe_high = sem("moe_high")
        moe_split = sem("moe_split")
        t2_done = sem("t2_done")
        t2_high = sem("t2_high")
        t2_split = sem("t2_split")
        gate_done = sem("gate_done")
        logits_ready = sem("logits_ready")
        top_ready = sem("top_ready")
        top_index = sem("top_index")
        top_step = sem("top_step")
        top_exp = sem("top_exp")
        gates_ready = sem("gates_ready")
        gates_high = sem("gates_high")
        gates_split = sem("gates_split")
        gt_done = sem("gt_done")
        gt_read = sem("gt_read")
        y_done = sem("y_done")
        y_added = sem("y_added")
        ew_high = sem("ew_high")
        ew_split = sem("ew_split")
        fin_stats = sem("fin_stats")
        fin_mom = sem("fin_mom")
        fin_eps = sem("fin_eps")
        fin_rstd = sem("fin_rstd")
        fin_ready = sem("fin_ready")
        w_loaded = {n: sem(f"w_loaded_{n}") for n in ("qkv", "o", "xkv", "xq", "xo")}
        ew_loaded = [sem(f"ew_loaded{i}") for i in range(2)]
        out_stored = [sem(f"out_stored{i}") for i in range(2)]

        banks = ctx.enter_context(nc.psum_tensor("banks", [P, 8, 512], F32))
        PJ = [banks[:, 0, :], banks[:, 1, :]]
        PT = [banks[:, 2, :], banks[:, 3, :]]
        PU = [banks[:, 4, :], banks[:, 5, :]]
        PO = [banks[:, 6, :], banks[:, 7, :]]
        PY = [banks[:, 4 + i, :] for i in range(YB)]

        x2_full = sb("x2", [P, B, D])
        x2 = x2_full[0:T]
        w_landing = x2_full[:].rearrange("p b d -> p (b d)")
        ident = sb("ident", [P, P])
        ident_r = sb("ident_r", [P, P], F32R)
        minus_half = sb("minus_half", [T, 1])
        eps_col = sb("eps_col", [T, 1])

        def three_passes(out, a_hi, a_lo, b_hi, b_lo, first=True, last=True):
            nc.tensor.matmul(out, a_hi, b_hi, start=first, stop=False)
            nc.tensor.matmul(out, a_hi, b_lo, start=False, stop=False)
            return nc.tensor.matmul(out, a_lo, b_hi, start=False, stop=last)

        def project(out, a_hi, a_lo, w_hi, w_lo, cols):
            for k in range(KC):
                mm = three_passes(out, a_hi[:, k, :], a_lo[:, k, :], w_hi[:, k, cols], w_lo[:, k, cols],
                                  k == 0, k == KC - 1)
            return mm

        with ExitStack() as attn:
            def asb(name, shape, dt=F32):
                return sb(name, shape, dt, attn)

            weights = [("qkv", w_qkv, KC, QKVW), ("o", w_o, KC, D), ("xkv", w_xkv, 1, 2 * D),
                       ("xq", w_xq, KC, D), ("xo", w_xo, KC, D)]
            w_order = {name: i for i, (name, *_) in enumerate(weights)}
            w_hi = {n: asb(f"w_{n}_hi", [P, kc, m], F32R) for n, _, kc, m in weights}
            w_lo = {n: asb(f"w_{n}_lo", [P, kc, m], F32R) for n, _, kc, m in weights}
            landing, at = {}, 0
            for n, _, kc, m in weights:
                if at + kc * m > B * D:
                    at = 0
                landing[n] = w_landing[:, at:at + kc * m].rearrange("p (c m) -> p c m", c=kc)
                at += kc * m

            bias_qkv = asb("bias_qkv", [T, QKVW])
            bias_o = asb("bias_o", [T, D])
            cos_t = asb("cos_t", [T, QKW])
            sin_t = asb("sin_t", [T, QKW])
            causal = asb("causal", [T, XC, T])
            prob_cap = asb("prob_cap", [T, XC, T])
            select_in = asb("select_in", [P, 2, T])
            select = asb("select", [P, 2, T], F32R)
            xin = asb("xin", [T, D])
            xres = asb("xres", [T, D])
            xT_in = asb("xT_in", [P, KC, T])
            xT_hi = asb("xT_hi", [P, KC, T], F32R)
            xT_lo = asb("xT_lo", [P, KC, T], F32R)
            qk = asb("qk", [T, QKW])
            rot_c = asb("rot_c", [T, QKW])
            rot_s = asb("rot_s", [T, QKW])
            q_parts = asb("q_parts", [T, HQ, 2, HD], F32R)
            k_parts = asb("k_parts", [T, 2, HKV, 2, HD], F32R)
            qT = asb("qT", [P, 2, J, T], F32R)
            kT = asb("kT", [P, 2, 2, T], F32R)
            v_aug = asb("v_aug", [T, HKV, HD + 1])
            row_max = asb("row_max", [T, J, P], F32R)
            maxT = asb("maxT", [P, J * T], F32R)
            probs = asb("probs", [T, 4, J, T])
            recip = asb("recip", [T, 2, HQ // 2])
            o_tok = asb("o_tok", [T, D])
            oT_hi = asb("oT_hi", [P, KC, T], F32R)
            oT_lo = asb("oT_lo", [P, KC, T], F32R)
            stats = asb("stats", [T, 6])
            moments = asb("moments", [T, 2])
            var_eps = asb("var_eps", [T, 1])
            rstd = asb("rstd", [T, 1])
            x1 = asb("x1", [T, D])
            x1_old = asb("x1_old", [T, D])
            cT_in = asb("cT_in", [P, T])
            cT_hi = asb("cT_hi", [P, T], F32R)
            cT_lo = asb("cT_lo", [P, T], F32R)
            x1T_hi = asb("x1T_hi", [P, KC, T], F32R)
            x1T_lo = asb("x1T_lo", [P, KC, T], F32R)
            xq_tok = asb("xq_tok", [T, D])
            xk_tok = asb("xk_tok", [T, D])
            xv_aug = asb("xv_aug", [T, XH, XD + 1])
            xqT_hi = asb("xqT_hi", [P, XC, T], F32R)
            xqT_lo = asb("xqT_lo", [P, XC, T], F32R)
            xkT_hi = asb("xkT_hi", [P, XC, T], F32R)
            xkT_lo = asb("xkT_lo", [P, XC, T], F32R)
            masked = asb("masked", [T, XC, T])
            xrow_max = asb("xrow_max", [T, XC, P], F32R)
            xmaxT = asb("xmaxT", [P, XC * T], F32R)
            xrecip = asb("xrecip", [T, 2, XH // 2])
            ox_tok = asb("ox_tok", [T, D])
            oxT_hi = asb("oxT_hi", [P, KC, T], F32R)
            oxT_lo = asb("oxT_lo", [P, KC, T], F32R)
            ystats = asb("ystats", [T, 6])
            ymoments = asb("ymoments", [T, 2])
            yvar_eps = asb("yvar_eps", [T, 1])
            yrstd = asb("yrstd", [T, 1])

            def chunked(src):
                return src.rearrange("(c p) n -> p c n", p=P)

            def pipeline(eng, step):
                for it in range(3):
                    step(it, True, it >= 1, it >= 2, True)
                with eng.Fori(3, B - 1) as it:
                    step(it, True, True, True, True)
                step(B - 1, True, True, True, False)
                step(B, False, True, True, False)
                step(B + 1, False, False, True, False)

            with nc.Block() as block:

                @block.sync
                def _(sp):
                    def load_weight(n, src):
                        sp.dma_start(landing[n], chunked(src)).then_inc(w_loaded[n], 16)

                    def load_xT(b):
                        sp.wait_ge(x_split, b)
                        sp.dma_start(xT_in[:], xT.rearrange("(c p) (b t) -> b p c t", p=P, t=T)[b])\
                          .then_inc(xT_loaded, 16)

                    def load_xin(b):
                        sp.wait_ge(xres_ready, b)
                        sp.dma_start(xin[:], x[b]).then_inc(xin_loaded, 16)

                    def load_ctx(b):
                        sp.wait_ge(c_split, b)
                        sp.dma_start(cT_in[:], ctxT.rearrange("p (b t) -> b p t", t=T)[b])\
                          .then_inc(ctx_loaded, 16)

                    load_xT(0)
                    load_weight("qkv", w_qkv)
                    for dst, src in ((ident, ident_c), (bias_qkv, b_qkv), (cos_t, rope_cos), (sin_t, rope_sin),
                                     (bias_o, b_o), (select_in, select_c), (causal, causal_c), (prob_cap, prob_cap_c)):
                        sp.dma_start(dst[:], src).then_inc(const_loaded, 16)
                    load_xin(0)
                    load_ctx(0)
                    for n, src, _, _ in weights[1:-1]:
                        load_weight(n, src)
                    sp.wait_ge(w_ready, 1)
                    load_weight("xo", w_xo)

                    def step(it, self_, cross, outp, more):
                        if more:
                            load_xT(it + 1)
                            load_xin(it + 1)
                            load_ctx(it + 1)
                    pipeline(sp, step)

                @block.scalar
                def _(act):
                    def copy(dst, src):
                        return nc.scalar.activation(dst, src, ACT.Copy)

                    def split_weight(n):
                        act.wait_ge(w_loaded[n], 16)
                        copy(w_hi[n][:], landing[n]).then_inc(w_high, 1)

                    def split_x(b):
                        act.wait_ge(xT_loaded, 16 * b + 16)
                        act.wait_ge(kv_done, b)
                        copy(xT_hi[:], xT_in[:]).then_inc(x_high, 1)

                    split_x(0)
                    split_weight("qkv")
                    act.wait_ge(const_loaded, 16 * 8)
                    copy(ident_r[:], ident[:]).then_inc(const_ready, 1)
                    copy(select[:], select_in[:]).then_inc(const_ready, 1)

                    def step(it, self_, cross, outp, more):
                        b, c = it, it - 1
                        if cross:
                            act.wait_ge(x1t_done, c + 1)
                            copy(x1T_hi[:], PT[0][:, 0:KC * T]).then_inc(x1t_high, 1)
                            act.wait_ge(xk_done, c + 1)
                            copy(xk_tok[:], PJ[1][0:T, :]).then_inc(xk_copied, 1)
                        if self_:
                            act.wait_ge(roped, b + 1)
                            copy(q_parts[:, :, 0, :], qk[:, 0:D].rearrange("t (h d) -> t h d", d=HD))\
                                .then_inc(qk_high, 1)
                            for dup in range(2):
                                copy(k_parts[:, 0, :, dup, :], qk[:, D:QKW].rearrange("t (h d) -> t h d", d=HD))\
                                    .then_inc(qk_high, 1)
                        if cross:
                            act.wait_ge(xq_done, c + 1)
                            copy(xq_tok[:], PJ[0][0:T, :]).then_inc(xq_copied, 1)
                        if self_:
                            for n, dst in enumerate((qT[:, 0], qT[:, 1], kT[:])):
                                act.wait_ge(tqk_done, 3 * b + n + 1)
                                copy(dst, PT[(1, 0, 1)[n]][:, 0:4 * T]).then_inc(tqk_read, 1)
                        if cross:
                            act.wait_ge(xqt_done, c + 1)
                            copy(xqT_hi[:], PT[0][:, 0:XC * T]).then_inc(xqt_high, 1)
                            act.wait_ge(xkt_done, c + 1)
                            copy(xkT_hi[:], PT[1][:, 0:XC * T]).then_inc(xkt_high, 1)
                            act.wait_ge(yres_added, c)
                            copy(x1_old[:], x1[:]).then_inc(x1_kept, 1)
                        if self_:
                            act.wait_ge(mt_done, b + 1)
                            copy(maxT[:], PT[0][:, 0:J * T]).then_inc(mt_read, 1)
                        if cross:
                            act.wait_ge(mxt_done, c + 1)
                            copy(xmaxT[:], PT[1][:, 0:XC * T]).then_inc(mxt_read, 1)
                        if self_:
                            for u in range(HKV):
                                act.wait_ge(st_done, 8 * b + u + 1)
                                if u >= 4:
                                    act.wait_ge(pv_done, 8 * b + u - 3)
                                elif outp:
                                    act.wait_ge(pvx_done, 4 * it - 7 + u)
                                nc.scalar.activation(probs[:, u % 4], PU[u % 2][0:T, 0:J * T], ACT.Exp,
                                                     scale=SELF_SCALE).then_inc(exp_done, 1)
                        if cross:
                            for i in range(XC):
                                act.wait_ge(stx_done, 4 * c + i + 1)
                                if self_:
                                    act.wait_ge(pv_done, 8 * b + 4 + i + 1)
                                else:
                                    act.wait_ge(pvx_done, 4 * c + i - 3)
                                nc.scalar.activation(probs[:, i], PU[i % 2][0:T, 0:XC * T], ACT.Exp,
                                                     scale=CROSS_SCALE).then_inc(expx_done, 1)
                        if isinstance(it, int) and it == 0:
                            for n in ("o", "xkv", "xq"):
                                split_weight(n)
                        if isinstance(it, int) and it == 1:
                            split_weight("xo")
                        if self_:
                            act.wait_ge(ot_done, b + 1)
                            copy(oT_hi[:], PT[0][:, 0:KC * T]).then_inc(ot_high, 1)
                        if cross:
                            act.wait_ge(oxt_done, c + 1)
                            copy(oxT_hi[:], PT[1][:, 0:KC * T]).then_inc(oxt_high, 1)
                        if self_:
                            act.wait_ge(ctx_loaded, 16 * b + 16)
                            copy(cT_hi[:], cT_in[:]).then_inc(c_high, 1)
                        if more:
                            split_x(b + 1)
                    pipeline(act, step)

                @block.gpsimd
                def _(pool):
                    def split_x(b):
                        pool.wait_ge(x_high, b + 1)
                        nc.gpsimd.tensor_tensor(xT_lo[:], xT_in[:], xT_hi[:].bitcast(F32), ALU.subtract)\
                            .then_inc(x_split, 1)

                    nc.gpsimd.memset(row_max[:].bitcast(F32), 0.0).then_inc(const_ready, 1)
                    nc.gpsimd.memset(xrow_max[:].bitcast(F32), 0.0).then_inc(const_ready, 1)
                    nc.gpsimd.memset(v_aug[:], 1.0).then_inc(const_ready, 1)
                    nc.gpsimd.memset(xv_aug[:], 1.0).then_inc(const_ready, 1)
                    nc.gpsimd.memset(minus_half[:], -0.5).then_inc(const_ready, 1)
                    nc.gpsimd.memset(eps_col[:], EPS).then_inc(const_ready, 1)
                    split_x(0)
                    pool.wait_ge(const_loaded, 16 * 8)
                    pool.wait_ge(const_ready, 8)

                    def step(it, self_, cross, outp, more):
                        b, c, y = it, it - 1, it - 2
                        if self_:
                            pool.wait_ge(xin_loaded, 16 * b + 16)
                            pool.wait_ge(res_added, b)
                            nc.gpsimd.tensor_tensor(xres[:], xin[:], bias_o[:], ALU.add).then_inc(xres_ready, 1)
                            pool.wait_ge(k_ready, b + 1)
                            pool.wait_ge(roped, b)
                            nc.gpsimd.tensor_tensor(rot_c[:], qk[:], cos_t[:], ALU.mult).then_inc(roped_cos, 1)
                        if outp:
                            pool.wait_ge(ymom_done, y + 1)
                            nc.gpsimd.tensor_tensor(yvar_eps[:], ymoments[:, 1:2], eps_col[:], ALU.add)\
                                .then_inc(yeps_done, 1)
                            pool.wait_ge(yeps_done, y + 1)
                            nc.gpsimd.tensor_tensor(yrstd[:], yvar_eps[:], minus_half[:], ALU.pow)\
                                .then_inc(yrstd_done, 1)
                        if self_:
                            pool.wait_ge(c_high, b + 1)
                            nc.gpsimd.tensor_tensor(cT_lo[:], cT_in[:], cT_hi[:].bitcast(F32), ALU.subtract)\
                                .then_inc(c_split, 1)
                        if more:
                            split_x(b + 1)
                        if self_:
                            pool.wait_ge(mom_done, b + 1)
                            nc.gpsimd.tensor_tensor(var_eps[:], moments[:, 1:2], eps_col[:], ALU.add)\
                                .then_inc(eps_done, 1)
                            pool.wait_ge(eps_done, b + 1)
                            nc.gpsimd.tensor_tensor(rstd[:], var_eps[:], minus_half[:], ALU.pow)\
                                .then_inc(rstd_done, 1)
                    pipeline(pool, step)

                @block.vector
                def _(dve):
                    v = nc.vector

                    def low_part(dst, src, hi):
                        return v.tensor_tensor(dst, src, hi.bitcast(F32), ALU.subtract)

                    def split_weight(n):
                        dve.wait_ge(w_high, w_order[n] + 1)
                        low_part(w_lo[n][:], landing[n], w_hi[n][:]).then_inc(w_ready, 1)

                    split_weight("qkv")
                    dve.wait_ge(const_ready, 8)
                    dve.wait_ge(const_loaded, 16 * 8)

                    def step(it, self_, cross, outp, more):
                        b, c, y = it, it - 1, it - 2
                        if self_:
                            dve.wait_ge(q_done, b + 1)
                            v.tensor_tensor(qk[:, 0:D], PJ[0][0:T, :], bias_qkv[:, 0:D], ALU.add)\
                                .then_inc(q_ready, 1)
                            dve.wait_ge(kv_done, b + 1)
                            v.tensor_tensor(qk[:, D:QKW], PJ[1][0:T, 0:KVW], bias_qkv[:, D:QKW], ALU.add)\
                                .then_inc(k_ready, 1)
                            v.tensor_tensor(v_aug[:, :, 0:HD],
                                            PJ[1][0:T, KVW:2 * KVW].rearrange("t (h d) -> t h d", d=HD),
                                            bias_qkv[:, QKW:QKVW].rearrange("t (h d) -> t h d", d=HD),
                                            ALU.add).then_inc(kv_ready, 1)
                            dve.wait_ge(q_ready, b + 1)
                            dve.wait_ge(k_ready, b + 1)
                            halves = [t.rearrange("t (h s d) -> t h s d", s=2, d=HD // 2)
                                      for t in (rot_s[:], qk[:], sin_t[:])]
                            for s in range(2):
                                v.tensor_tensor(halves[0][:, :, s], halves[1][:, :, 1 - s], halves[2][:, :, s],
                                                ALU.mult).then_inc(roped_sin, 1)
                        if cross:
                            dve.wait_ge(x1t_high, c + 1)
                            low_part(x1T_lo[:], PT[0][:, 0:KC * T].rearrange("p (c t) -> p c t", c=KC), x1T_hi[:]).then_inc(x1t_split, 1)
                        if self_:
                            dve.wait_ge(roped_sin, 2 * b + 2)
                            dve.wait_ge(roped_cos, b + 1)
                            v.tensor_tensor(qk[:], rot_c[:], rot_s[:], ALU.add).then_inc(roped, 1)
                            dve.wait_ge(qk_high, 3 * b + 3)
                            low_part(q_parts[:, :, 1, :], qk[:, 0:D].rearrange("t (h d) -> t h d", d=HD),
                                     q_parts[:, :, 0, :]).then_inc(qk_split, 1)
                            for dup in range(2):
                                low_part(k_parts[:, 1, :, dup, :], qk[:, D:QKW].rearrange("t (h d) -> t h d", d=HD),
                                         k_parts[:, 0, :, dup, :]).then_inc(qk_split, 1)
                        if cross:
                            dve.wait_ge(xv_done, c + 1)
                            v.tensor_copy(xv_aug[:, :, 0:XD], PJ[1][0:T, :].rearrange("t (h d) -> t h d", d=XD))\
                                .then_inc(xv_copied, 1)
                            dve.wait_ge(xqt_high, c + 1)
                            low_part(xqT_lo[:], PT[0][:, 0:XC * T].rearrange("p (c t) -> p c t", c=XC), xqT_hi[:]).then_inc(xqt_split, 1)
                            dve.wait_ge(xkt_high, c + 1)
                            low_part(xkT_lo[:], PT[1][:, 0:XC * T].rearrange("p (c t) -> p c t", c=XC), xkT_hi[:]).then_inc(xkt_split, 1)
                        if outp:
                            dve.wait_ge(wxo_done, y + 1)
                            dve.wait_ge(x1_kept, y + 1)
                            v.tensor_tensor(ox_tok[:], PJ[0][0:T, :], x1_old[:], ALU.add).then_inc(yres_added, 1)
                            dve.wait_ge(yres_added, y + 1)
                            v.bn_stats(ystats[:], ox_tok[:]).then_inc(ystats_done, 1)
                            dve.wait_ge(const_ready, 8)
                            dve.wait_ge(ystats_done, y + 1)
                            v.bn_aggr(ymoments[:], ystats[:]).then_inc(ymom_done, 1)
                        if self_:
                            for g in range(HKV):
                                dve.wait_ge(s_done, 8 * b + g + 1)
                                col = 32 * (g % 4) + g // 4
                                v.reduce_max(row_max[:, :, col], PU[g % 2][0:T, 0:J * T].rearrange("q (j k) -> q j k", j=J),
                                             AX_X).then_inc(s_max, 1)
                        if outp:
                            dve.wait_ge(yrstd_done, y + 1)
                            v.tensor_scalar(x2[:, y, :], ox_tok[:], ymoments[:, 0:1], yrstd[:], ALU.subtract, ALU.mult)\
                                .then_inc(x2_ready, 1)
                        if cross:
                            for i in range(XC):
                                dve.wait_ge(sx_done, 4 * c + i + 1)
                                dve.wait_ge(sx_max, 4 * c + i)
                                v.tensor_tensor(masked[:], PU[i % 2][0:T, 0:XC * T].rearrange("q (c k) -> q c k", c=XC),
                                                causal[:], ALU.add).then_inc(sx_masked, 1)
                                dve.wait_ge(sx_masked, 4 * c + i + 1)
                                v.reduce_max(xrow_max[:, :, 32 * i], masked[:], AX_X).then_inc(sx_max, 1)
                        if self_:
                            for half in range(2):
                                sums = PO[half][0:T, 0:16 * (HD + 1)].rearrange("q (h d) -> q h d", d=HD + 1)
                                dve.wait_ge(pv_done, 8 * b + 4 * half + 4)
                                v.reciprocal(recip[:, half, :], sums[:, :, HD]).then_inc(recip_done, 1)
                                dve.wait_ge(recip_done, 2 * b + half + 1)
                                v.tensor_tensor(o_tok[:, half * 256:half * 256 + 256].rearrange("q (h d) -> q h d", d=HD),
                                                sums[:, :, 0:HD], recip[:, half, :].unsqueeze(2).to_broadcast([T, 16, HD]),
                                                ALU.mult).then_inc(self_norm, 1)
                        if cross:
                            for i in range(XC):
                                dve.wait_ge(expx_done, 4 * c + i + 1)
                                v.tensor_tensor(probs[:, i], probs[:, i], prob_cap[:], ALU.min)\
                                    .then_inc(px_masked, 1)
                            for half in range(2):
                                sums = PO[half][0:T, 0:8 * (XD + 1)].rearrange("q (h d) -> q h d", d=XD + 1)
                                dve.wait_ge(pvx_done, 4 * c + 2 * half + 2)
                                v.reciprocal(xrecip[:, half, :], sums[:, :, XD]).then_inc(xrecip_done, 1)
                                dve.wait_ge(xrecip_done, 2 * c + half + 1)
                                v.tensor_tensor(ox_tok[:, half * 256:half * 256 + 256].rearrange("q (h d) -> q h d", d=XD),
                                                sums[:, :, 0:XD], xrecip[:, half, :].unsqueeze(2).to_broadcast([T, 8, XD]),
                                                ALU.mult).then_inc(cross_norm, 1)
                        if isinstance(it, int) and it == 0:
                            for n in ("o", "xkv", "xq"):
                                split_weight(n)
                        if isinstance(it, int) and it == 1:
                            split_weight("xo")
                        if self_:
                            dve.wait_ge(ot_high, b + 1)
                            low_part(oT_lo[:], PT[0][:, 0:KC * T].rearrange("p (c t) -> p c t", c=KC), oT_hi[:]).then_inc(ot_split, 1)
                        if cross:
                            dve.wait_ge(oxt_high, c + 1)
                            low_part(oxT_lo[:], PT[1][:, 0:KC * T].rearrange("p (c t) -> p c t", c=KC), oxT_hi[:]).then_inc(oxt_split, 1)
                        if self_:
                            dve.wait_ge(wo_done, b + 1)
                            dve.wait_ge(xres_ready, b + 1)
                            v.tensor_tensor(o_tok[:], PJ[1][0:T, :], xres[:], ALU.add).then_inc(res_added, 1)
                            dve.wait_ge(res_added, b + 1)
                            v.bn_stats(stats[:], o_tok[:]).then_inc(stats_done, 1)
                            dve.wait_ge(const_ready, 8)
                            dve.wait_ge(stats_done, b + 1)
                            v.bn_aggr(moments[:], stats[:]).then_inc(mom_done, 1)
                            dve.wait_ge(rstd_done, b + 1)
                            dve.wait_ge(x1_kept, b)
                            v.tensor_scalar(x1[:], o_tok[:], moments[:, 0:1], rstd[:], ALU.subtract, ALU.mult)\
                                .then_inc(x1_ready, 1)
                    pipeline(dve, step)

                @block.tensor
                def _(pe):
                    mm = nc.tensor.matmul

                    def transposed(bank, tok):
                        for k in range(KC):
                            last = nc.tensor.transpose(bank[:, k * T:(k + 1) * T], tok[:, k * P:(k + 1) * P], ident[0:T, 0:T])
                        return last

                    pe.wait_ge(const_ready, 8)
                    pe.wait_ge(const_loaded, 16 * 8)

                    def step(it, self_, cross, outp, more):
                        b, c, y = it, it - 1, it - 2
                        if self_:
                            if isinstance(it, int) and it == 0:
                                pe.wait_ge(w_ready, w_order["qkv"] + 1)
                            pe.wait_ge(x_split, b + 1)
                            if outp:
                                pe.wait_ge(yres_added, b - 2)
                            project(PJ[0][0:T, :], xT_hi, xT_lo, w_hi["qkv"], w_lo["qkv"], slice(0, D))\
                                .then_inc(q_done, 1)
                            pe.wait_ge(res_added, b)
                            project(PJ[1][0:T, 0:2 * KVW], xT_hi, xT_lo, w_hi["qkv"], w_lo["qkv"], slice(D, QKVW))\
                                .then_inc(kv_done, 1)
                        if cross:
                            pe.wait_ge(x1_ready, c + 1)
                            transposed(PT[0], x1).then_inc(x1t_done, 1)
                            if isinstance(it, int) and it == 1:
                                pe.wait_ge(w_ready, w_order["xkv"] + 1)
                            pe.wait_ge(c_split, c + 1)
                            if self_:
                                pe.wait_ge(kv_ready, b + 1)
                            three_passes(PJ[1][0:T, :], cT_hi[:], cT_lo[:], w_hi["xkv"][:, 0, 0:D], w_lo["xkv"][:, 0, 0:D])\
                                .then_inc(xk_done, 1)
                            if isinstance(it, int) and it == 1:
                                pe.wait_ge(w_ready, w_order["xq"] + 1)
                            pe.wait_ge(x1t_split, c + 1)
                            if self_:
                                pe.wait_ge(q_ready, b + 1)
                            project(PJ[0][0:T, :], x1T_hi, x1T_lo, w_hi["xq"], w_lo["xq"], slice(0, D))\
                                .then_inc(xq_done, 1)
                            pe.wait_ge(xk_copied, c + 1)
                            three_passes(PJ[1][0:T, :], cT_hi[:], cT_lo[:], w_hi["xkv"][:, 0, D:2 * D],
                                         w_lo["xkv"][:, 0, D:2 * D]).then_inc(xv_done, 1)
                        if self_:
                            pe.wait_ge(qk_split, 3 * b + 3)
                            parts = [q_parts[:].rearrange("t h s d -> t (h s d)")[:, n * P:(n + 1) * P] for n in range(8)]
                            parts += [k_parts[:].rearrange("t s h u d -> t (s h u d)")[:, n * P:(n + 1) * P] for n in range(4)]
                            for n in range(3):
                                if n == 0 and cross:
                                    pe.wait_ge(oxt_split, b - 1)
                                elif n == 2:
                                    pe.wait_ge(tqk_read, 3 * b + 1)
                                for m in range(4):
                                    last = mm(PT[(1, 0, 1)[n]][:, m * T:(m + 1) * T], parts[4 * n + m], ident_r[0:T, 0:T],
                                              start=True, stop=True)
                                last.then_inc(tqk_done, 1)
                        if cross:
                            pe.wait_ge(xq_copied, c + 1)
                            if self_:
                                pe.wait_ge(tqk_read, 3 * b + 2)
                            transposed(PT[0], xq_tok).then_inc(xqt_done, 1)
                            if self_:
                                pe.wait_ge(tqk_read, 3 * b + 3)
                            else:
                                pe.wait_ge(oxt_split, c)
                            transposed(PT[1], xk_tok).then_inc(xkt_done, 1)
                        if outp:
                            if isinstance(it, int) and it == 2:
                                pe.wait_ge(w_ready, w_order["xo"] + 1)
                            pe.wait_ge(oxt_split, y + 1)
                            project(PJ[0][0:T, :], oxT_hi, oxT_lo, w_hi["xo"], w_lo["xo"], slice(0, D))\
                                .then_inc(wxo_done, 1)
                        if self_:
                            pe.wait_ge(tqk_read, 3 * b + 3)
                            for g in range(HKV):
                                rows, gh = slice(32 * (g % 4), 32 * (g % 4) + 32), g // 4
                                if g >= 2:
                                    pe.wait_ge(s_max, 8 * b + g - 1)
                                for j in range(J):
                                    last = mm(PU[g % 2][0:T, j * T:(j + 1) * T], qT[rows, gh, j, :], kT[rows, 0, gh, :],
                                              start=True, stop=True)
                                last.then_inc(s_done, 1)
                        if cross:
                            pe.wait_ge(xqt_high, c + 1)
                            pe.wait_ge(xkt_high, c + 1)
                            for i in range(XC):
                                rows = slice(32 * i, 32 * i + 32)
                                if i >= 2:
                                    pe.wait_ge(sx_masked, 4 * c + i - 1)
                                elif self_:
                                    pe.wait_ge(s_max, 8 * b + 7 + i)
                                for h in range(XC):
                                    last = mm(PU[i % 2][0:T, h * T:(h + 1) * T], xqT_hi[rows, h, :], xkT_hi[rows, h, :],
                                              start=True, stop=True)
                                last.then_inc(sx_done, 1)
                        if self_:
                            pe.wait_ge(s_max, 8 * b + 8)
                            if cross:
                                pe.wait_ge(xqt_split, c + 1)
                            for j in range(J):
                                last = mm(PT[0][:, j * T:(j + 1) * T], row_max[:, j, :], ident_r[0:T, 0:T], start=True, stop=True)
                            last.then_inc(mt_done, 1)
                        if cross:
                            pe.wait_ge(sx_max, 4 * c + 4)
                            pe.wait_ge(xkt_split, c + 1)
                            for h in range(XC):
                                last = mm(PT[1][:, h * T:(h + 1) * T], xrow_max[:, h, :], ident_r[0:T, 0:T], start=True, stop=True)
                            last.then_inc(mxt_done, 1)
                        if self_:
                            def scores_t(g):
                                rows, gh, bank = slice(32 * (g % 4), 32 * (g % 4) + 32), g // 4, PU[g % 2][0:T, 0:J * T]
                                mm(bank, select[rows, gh, :], maxT[rows, :], start=True, stop=False)
                                mm(bank, kT[rows, 0, gh, :], qT[rows, gh], start=False, stop=False)
                                mm(bank, kT[rows, 1, gh, :], qT[rows, gh], start=False, stop=True)\
                                    .then_inc(st_done, 1)

                            def values(g):
                                pe.wait_ge(exp_done, 8 * b + g + 1)
                                for j in range(J):
                                    at = ((g % 4) * J + j) * (HD + 1)
                                    last = mm(PO[g // 4][0:T, at:at + HD + 1], probs[:, g % 4, j, :], v_aug[:, g, :],
                                              start=True, stop=True)
                                last.then_inc(pv_done, 1)

                            pe.wait_ge(mt_read, b + 1)
                            scores_t(0)
                            for g in range(1, HKV):
                                scores_t(g)
                                values(g - 1)
                            values(HKV - 1)
                        if cross:
                            def cross_scores_t(i):
                                rows, bank = slice(32 * i, 32 * i + 32), PU[i % 2][0:T]
                                mm(bank[:, 0:XC * T], select[rows, 0, :], xmaxT[rows, :], start=True, stop=False)
                                for h in range(XC):
                                    last = three_passes(bank[:, h * T:(h + 1) * T], xkT_hi[rows, h, :], xkT_lo[rows, h, :],
                                                        xqT_hi[rows, h, :], xqT_lo[rows, h, :], False, h == XC - 1)
                                last.then_inc(stx_done, 1)

                            def cross_values(i):
                                pe.wait_ge(px_masked, 4 * c + i + 1)
                                if self_ and i % 2 == 0:
                                    pe.wait_ge(self_norm, 2 * b + i // 2 + 1)
                                for h in range(XC):
                                    at = ((i % 2) * XC + h) * (XD + 1)
                                    last = mm(PO[i // 2][0:T, at:at + XD + 1], probs[:, i, h, :], xv_aug[:, XC * i + h, :],
                                              start=True, stop=True)
                                last.then_inc(pvx_done, 1)

                            pe.wait_ge(mxt_read, c + 1)
                            cross_scores_t(0)
                            for i in range(1, XC):
                                cross_scores_t(i)
                                cross_values(i - 1)
                            cross_values(XC - 1)
                        if self_:
                            pe.wait_ge(self_norm, 2 * b + 2)
                            transposed(PT[0], o_tok).then_inc(ot_done, 1)
                        if cross:
                            pe.wait_ge(cross_norm, 2 * c + 2)
                            transposed(PT[1], ox_tok).then_inc(oxt_done, 1)
                        if self_:
                            if isinstance(it, int) and it == 0:
                                pe.wait_ge(w_ready, w_order["o"] + 1)
                            pe.wait_ge(ot_split, b + 1)
                            pe.wait_ge(kv_ready, b + 1)
                            if cross:
                                pe.wait_ge(xv_copied, c + 1)
                            project(PJ[1][0:T, :], oT_hi, oT_lo, w_hi["o"], w_lo["o"], slice(0, D))\
                                .then_inc(wo_done, 1)
                    pipeline(pe, step)

        x2T_hi = sb("x2T_hi", [P, B, KC, T], F32R)
        x2T_lo = sb("x2T_lo", [P, B, KC, T], F32R)
        ew_in = [sb(f"ew_in{i}", [P, KC, D]) for i in range(2)]
        ew_hi = [sb(f"ew_hi{i}", [P, KC, D], F32R) for i in range(2)]
        ew_lo = [sb(f"ew_lo{i}", [P, KC, D], F32R) for i in range(2)]
        gate_in = sb("gate_in", [P, KC, E])
        gate_hi = sb("gate_hi", [P, KC, E], F32R)
        gate_lo = sb("gate_lo", [P, KC, E], F32R)
        eb_in = sb("eb_in", [2 * E, D])
        eb_hi = sb("eb_hi", [2 * E, D], F32R)
        eb_lo = sb("eb_lo", [2 * E, D], F32R)
        ids = sb("ids", [T, E])
        logits = sb("logits", [T, B, E])
        top = sb("top", [T, B, 8])
        top_at = sb("top_at", [T, B, 8], U32)
        top_atf = sb("top_atf", [T, B, 2])
        diff = sb("diff", [T, B])
        ex = sb("ex", [T, B])
        denom = sb("denom", [T, B])
        share = sb("share", [T, 2, B])
        pick = sb("pick", [T, 2, B, E])
        gates = sb("gates", [T, B, E])
        g_parts = sb("g_parts", [T, B, P], F32R)
        gT = sb("gT", [2 * E, 2, T], F32R)
        fstats = sb("fstats", [T, 2, 6])
        fmoments = sb("fmoments", [T, 2, 2])
        fvar = sb("fvar", [T, 2])
        frstd = sb("frstd", [T, 2])
        fin = sb("fin", [T, 2, D])

        with nc.Block() as block:

            @block.sync
            def _(sp):
                def load_expert(e, slot):
                    sp.dma_start(ew_in[slot][:], w_exp.rearrange("e (c p) n -> e p c n", p=P)[e]).then_inc(ew_loaded[slot], 16)

                load_expert(0, 0)
                sp.dma_start(gate_in[:], w_gate.rearrange("(c p) e -> p c e", p=P)).then_inc(moe_loaded, 16)
                sp.dma_start(eb_in[0:E, :], b_exp).then_inc(moe_loaded, 16)
                sp.dma_start(eb_in[E:2 * E, :], b_exp).then_inc(moe_loaded, 16)
                sp.dma_start(ids[:], expert_ids_c).then_inc(moe_loaded, 16)
                load_expert(1, 1)
                with sp.Fori(1, E // 2) as pair:
                    e = pair * 2
                    for slot in range(2):
                        sp.wait_ge(ew_split, e + slot - 1)
                        load_expert(e + slot, slot)
                for b in range(B):
                    sp.wait_ge(fin_ready, b + 1)
                    sp.dma_start(out[b], fin[:, b % 2, :]).then_inc(out_stored[b % 2], 16)
                sp.wait_ge(out_stored[0], 16 * B // 2)
                sp.wait_ge(out_stored[1], 16 * B // 2)

            @block.scalar
            def _(act):
                def copy(dst, src):
                    return nc.scalar.activation(dst, src, ACT.Copy)

                def high_expert(slot, nth):
                    act.wait_ge(ew_loaded[slot], 16 * nth)
                    copy(ew_hi[slot][:], ew_in[slot][:]).then_inc(ew_high, 1)

                act.wait_ge(moe_loaded, 64)
                copy(gate_hi[:], gate_in[:]).then_inc(moe_high, 1)
                copy(eb_hi[:], eb_in[:]).then_inc(moe_high, 1)
                for b in range(B + 1):
                    if b < B:
                        act.wait_ge(t2_done, b + 1)
                        copy(x2T_hi[:, b], PT[b % 2][:, 0:KC * T]).then_inc(t2_high, 1)
                    if b >= 1:
                        act.wait_ge(gate_done, b)
                        copy(logits[:, b - 1, :], PJ[(b - 1) % 2][0:T, 0:E]).then_inc(logits_ready, 1)
                    if b == 4:
                        high_expert(0, 1)
                    if b == 8:
                        high_expert(1, 1)
                act.wait_ge(top_step, 1)
                nc.scalar.activation(ex[:], diff[:], ACT.Exp).then_inc(top_exp, 1)
                act.wait_ge(gates_ready, 1)
                copy(g_parts[:, :, 0:E], gates[:]).then_inc(gates_high, 1)
                for b in range(B):
                    act.wait_ge(gt_done, b + 1)
                    copy(gT[:, b % 2, :], PT[b % 2][0:2 * E, 0:T]).then_inc(gt_read, 1)
                with act.Fori(1, E // 2) as pair:
                    e = pair * 2
                    for slot in range(2):
                        act.wait_ge(y_done, B * (e + slot))
                        high_expert(slot, pair + 1)

            @block.gpsimd
            def _(pool):
                def low_expert(e, slot):
                    pool.wait_ge(ew_high, e + 1)
                    nc.gpsimd.tensor_tensor(ew_lo[slot][:], ew_in[slot][:], ew_hi[slot][:].bitcast(F32), ALU.subtract)\
                        .then_inc(ew_split, 1)

                nc.gpsimd.memset(g_parts[:].bitcast(F32), 0.0).then_inc(moe_split, 1)
                pool.wait_ge(moe_high, 2)
                nc.gpsimd.tensor_tensor(gate_lo[:], gate_in[:], gate_hi[:].bitcast(F32), ALU.subtract)\
                    .then_inc(moe_split, 1)
                nc.gpsimd.tensor_tensor(eb_lo[:], eb_in[:], eb_hi[:].bitcast(F32), ALU.subtract)\
                    .then_inc(moe_split, 1)
                low_expert(0, 0)
                low_expert(1, 1)
                with pool.Fori(1, E // 2) as pair:
                    e = pair * 2
                    for slot in range(2):
                        low_expert(e + slot, slot)
                for b in range(B):
                    pool.wait_ge(fin_eps, b + 1)
                    nc.gpsimd.tensor_tensor(frstd[:, b % 2:b % 2 + 1], fvar[:, b % 2:b % 2 + 1], minus_half[:], ALU.pow)\
                        .then_inc(fin_rstd, 1)

            @block.vector
            def _(dve):
                v = nc.vector
                for b in range(B + 1):
                    if b < B:
                        dve.wait_ge(t2_high, b + 1)
                        v.tensor_tensor(x2T_lo[:, b], PT[b % 2][:, 0:KC * T].rearrange("p (c t) -> p c t", c=KC),
                                        x2T_hi[:, b].bitcast(F32), ALU.subtract).then_inc(t2_split, 1)
                    if b >= 1:
                        dve.wait_ge(logits_ready, b)
                        v.max(top[:, b - 1, :], logits[:, b - 1, :]).then_inc(top_ready, 1)
                        dve.wait_ge(top_ready, b)
                        v.max_index(top_at[:, b - 1, :], top[:, b - 1, :], logits[:, b - 1, :]).then_inc(top_index, 1)
                v.tensor_tensor(diff[:], top[:, :, 1], top[:, :, 0], ALU.subtract).then_inc(top_step, 1)
                dve.wait_ge(top_index, B)
                v.tensor_copy(top_atf[:], top_at[:, :, 0:2]).then_inc(top_step, 1)
                dve.wait_ge(top_exp, 1)
                v.tensor_scalar(denom[:], ex[:], 1.0, None, ALU.add).then_inc(top_step, 1)
                dve.wait_ge(top_step, 3)
                v.reciprocal(share[:, 0, :], denom[:]).then_inc(top_step, 1)
                dve.wait_ge(top_step, 4)
                v.tensor_tensor(share[:, 1, :], ex[:], share[:, 0, :], ALU.mult).then_inc(top_step, 1)
                dve.wait_ge(moe_loaded, 64)
                for r in range(2):
                    v.tensor_tensor(pick[:, r], ids[:].unsqueeze(1).to_broadcast([T, B, E]),
                                    top_atf[:, :, r].unsqueeze(2).to_broadcast([T, B, E]), ALU.is_equal)\
                        .then_inc(top_step, 1)
                dve.wait_ge(top_step, 7)
                for r in range(2):
                    v.tensor_tensor(pick[:, r], pick[:, r], share[:, r, :].unsqueeze(2).to_broadcast([T, B, E]), ALU.mult)\
                        .then_inc(top_step, 1)
                dve.wait_ge(top_step, 9)
                v.tensor_tensor(gates[:], pick[:, 0], pick[:, 1], ALU.add).then_inc(gates_ready, 1)
                dve.wait_ge(gates_high, 1)
                v.tensor_tensor(g_parts[:, :, E:2 * E], gates[:], g_parts[:, :, 0:E].bitcast(F32), ALU.subtract)\
                    .then_inc(gates_split, 1)
                for b in range(B):
                    dve.wait_ge(y_done, b + 1)
                    v.tensor_tensor(x2[:, b, :], PY[b % YB][0:T, :], x2[:, b, :], ALU.add).then_inc(y_added, 1)

                def add_expert(e, b):
                    dve.wait_ge(y_done, B * e + B + b + 1)
                    dve.wait_ge(y_added, B * e + b + 1)
                    v.scalar_tensor_tensor(out=x2[:, b, :], in0=PY[b % YB][0:T, :], scalar=gates[:, b, bass.ds(e, 1)],
                                           in1=x2[:, b, :], op0=ALU.mult, op1=ALU.add).then_inc(y_added, 1)

                def normalise(b):
                    s = b % 2
                    dve.wait_ge(fin_rstd, b + 1)
                    dve.wait_ge(out_stored[s], 16 * (b // 2))
                    v.tensor_scalar(fin[:, s, :], x2[:, b, :], fmoments[:, s, 0:1], frstd[:, s:s + 1], ALU.subtract, ALU.mult)\
                        .then_inc(fin_ready, 1)

                with dve.Fori(0, E // 2 - 1) as pair:
                    e = pair * 2
                    for slot in range(2):
                        for b in range(B):
                            add_expert(e + slot, b)
                for b in range(B):
                    add_expert(E - 2, b)
                for b in range(B):
                    s = b % 2
                    add_expert(E - 1, b)
                    dve.wait_ge(y_added, B * E + b + 1)
                    v.bn_stats(fstats[:, s, :], x2[:, b, :]).then_inc(fin_stats, 1)
                    dve.wait_ge(fin_stats, b + 1)
                    v.bn_aggr(fmoments[:, s, :], fstats[:, s, :]).then_inc(fin_mom, 1)
                    dve.wait_ge(fin_mom, b + 1)
                    v.tensor_scalar(fvar[:, s:s + 1], fmoments[:, s, 1:2], EPS, None, ALU.add).then_inc(fin_eps, 1)
                    if b >= 1:
                        normalise(b - 1)
                normalise(B - 1)

            @block.tensor
            def _(pe):
                mm = nc.tensor.matmul
                for b in range(B + 1):
                    if b < B:
                        if b >= 2:
                            pe.wait_ge(t2_split, b - 1)
                        for k in range(KC):
                            last = nc.tensor.transpose(PT[b % 2][:, k * T:(k + 1) * T], x2[:, b, k * P:(k + 1) * P], ident[0:T, 0:T])
                        last.then_inc(t2_done, 1)
                    if b == 1:
                        pe.wait_ge(moe_split, 3)
                    if b >= 1:
                        pe.wait_ge(t2_split, b)
                        if b >= 3:
                            pe.wait_ge(logits_ready, b - 2)
                        project(PJ[(b - 1) % 2][0:T, 0:E], x2T_hi[:, b - 1], x2T_lo[:, b - 1], gate_hi, gate_lo, slice(0, E))\
                            .then_inc(gate_done, 1)
                pe.wait_ge(gates_split, 1)
                for b in range(B + 1):
                    if b < B:
                        if b >= 2:
                            pe.wait_ge(gt_read, b - 1)
                        mm(PT[b % 2][:, 0:T], g_parts[:, b, :], ident_r[0:T, 0:T], start=True, stop=True).then_inc(gt_done, 1)
                    if b >= 1:
                        pe.wait_ge(gt_read, b)
                        if b > YB:
                            pe.wait_ge(y_added, b - YB)
                        bank = PY[(b - 1) % YB][0:T, :]
                        mm(bank, gT[:, (b - 1) % 2, :], eb_hi[:], start=True, stop=False)
                        mm(bank, gT[:, (b - 1) % 2, :], eb_lo[:], start=False, stop=True).then_inc(y_done, 1)
                with pe.Fori(0, E // 2) as pair:
                    e = pair * 2
                    for slot in range(2):
                        pe.wait_ge(ew_split, e + slot + 1)
                        for b in range(B):
                            pe.wait_ge(y_added, B * (e + slot) + B + b - YB + 1)
                            project(PY[b % YB][0:T, :], x2T_hi[:, b], x2T_lo[:, b], ew_hi[slot], ew_lo[slot], slice(0, D))\
                                .then_inc(y_done, 1)


def kernel(x, ctx_512, L0_attn_Wq, L0_attn_bq, L0_attn_Wk, L0_attn_bk, L0_attn_Wv, L0_attn_bv, L0_attn_Wo, L0_attn_bo,
           L0_xattn_Wq, L0_xattn_Wkv_expand, L0_xattn_Wout, L0_ffn_gate_w, L0_ffn_expert_w, L0_ffn_expert_b):
    import numpy as np
    import concourse.bacc as bacc
    from concourse.bass_utils import run_bass_kernel_spmd

    def q_order(w):
        return w.reshape(2, 4, J, HD, -1).transpose(0, 2, 1, 3, 4).reshape(D, -1)

    def x_order(w):
        return w.reshape(4, XC, XD, -1).transpose(1, 0, 2, 3).reshape(D, -1)

    def rows(v):
        return np.broadcast_to(np.asarray(v)[None, :], (T, v.shape[0]))

    x, ctx = np.asarray(x), np.asarray(ctx_512)
    wq, bq = q_order(np.asarray(L0_attn_Wq)), q_order(np.asarray(L0_attn_bq)[:, None])[:, 0]
    wkv = np.asarray(L0_xattn_Wkv_expand)
    inv_freq = (1.0 / 10000.0 ** (np.arange(0, HD, 2, dtype=np.float32) / HD)).astype(np.float32)
    ang = np.arange(T, dtype=np.float32)[:, None] * inv_freq[None, :]
    cos, sin = np.cos(ang), np.sin(ang)
    select = np.zeros((P, 2, T), np.float32)
    for strip in range(4):
        for gh in range(2):
            select[32 * strip + gh, gh] = -1.0
    causal = np.where(np.arange(T)[None, :] <= np.arange(T)[:, None], 0.0, -1e30).astype(np.float32)
    cap = np.where(np.arange(T)[:, None] <= np.arange(T)[None, :], np.finfo(np.float32).max, 0.0).astype(np.float32)
    arrays = {
        "x": x,
        "xT": x.reshape(B * T, D).T,
        "ctxT": ctx[:, :T, :].reshape(B * T, P).T,
        "w_qkv": np.concatenate([wq, np.asarray(L0_attn_Wk), np.asarray(L0_attn_Wv)]).T,
        "b_qkv": rows(np.concatenate([bq, np.asarray(L0_attn_bk), np.asarray(L0_attn_bv)])),
        "w_o": np.asarray(L0_attn_Wo).T,
        "b_o": rows(L0_attn_bo),
        "w_xkv": np.concatenate([x_order(wkv[:D]), wkv[D:]]).T,
        "w_xq": x_order(np.asarray(L0_xattn_Wq)).T,
        "w_xo": np.asarray(L0_xattn_Wout).T,
        "w_gate": np.asarray(L0_ffn_gate_w).T,
        "w_exp": np.asarray(L0_ffn_expert_w),
        "b_exp": np.asarray(L0_ffn_expert_b),
        "rope_cos": np.tile(np.concatenate([cos, cos], 1), (1, QKW // HD)),
        "rope_sin": np.tile(np.concatenate([-sin, sin], 1), (1, QKW // HD)),
        "ident": np.eye(P, dtype=np.float32),
        "select": select,
        "causal": np.broadcast_to(causal[:, None, :], (T, XC, T)),
        "prob_cap": np.broadcast_to(cap[:, None, :], (T, XC, T)),
        "expert_ids": np.broadcast_to(np.arange(E, dtype=np.float32)[None, :], (T, E)),
    }
    arrays = {f"in_{k}": np.ascontiguousarray(v) for k, v in arrays.items()}
    nc = bacc.Bacc("TRN2", target_bir_lowering=False, num_devices=1)
    args = [nc.dram_tensor(k, v.shape, mybir.dt.from_np(v.dtype), kind="ExternalInput").ap() for k, v in arrays.items()]
    args.append(nc.dram_tensor("out", (B, T, D), F32, kind="ExternalOutput").ap())
    build_decoder(nc, *args)
    r = run_bass_kernel_spmd(nc, [arrays], core_ids=[0])
    return r.results[0]["out"]
```

```python
from contextlib import ExitStack

import concourse.bass as bass
from concourse import mybir

F32 = mybir.dt.float32
F32R = mybir.dt.float32r
U32 = mybir.dt.uint32
ALU = mybir.AluOpType
ACT = mybir.ActivationFunctionType
AX_X = mybir.AxisListType.X

B, T, D, P = 16, 100, 512, 128
KC = D // P
HQ, HKV, HD = 32, 8, 16
J = HQ // HKV
XH, XD = 16, 32
XC = 4
KVW = HKV * HD
QKW = D + KVW
QKVW = D + 2 * KVW
E = 8
EPS = 1e-5
SELF_SCALE = HD ** -0.5
CROSS_SCALE = XD ** -0.5
VPITCH = P + HD
XRECIPS = 1 + XC
YB = 4


def build_decoder(nc, x, xT, ctxT, w_qkv, b_qkv, w_o, b_o, w_xkv, w_xq, w_xo, w_gate, w_exp, b_exp,
                  rope_cos, rope_sin, ident_c, select_c, causal_c, causal_t_c, expert_ids_c, out):
    with ExitStack() as ctx:
        def sb(name, shape, dt=F32, stack=ctx):
            return stack.enter_context(nc.sbuf_tensor(name, shape, dt))

        def sem(name):
            return ctx.enter_context(nc.semaphore(name))

        const_loaded = sem("const_loaded")
        zeroed = sem("zeroed")
        const_ready = sem("const_ready")
        w_high = sem("w_high")
        w_ready = sem("w_ready")
        xT_loaded = sem("xT_loaded")
        xin_loaded = sem("xin_loaded")
        x_high = sem("x_high")
        x_split = sem("x_split")
        ctx_loaded = sem("ctx_loaded")
        c_high = sem("c_high")
        c_split = sem("c_split")
        xres_ready = sem("xres_ready")
        q_done = sem("q_done")
        kv_done = sem("kv_done")
        q_ready = sem("q_ready")
        k_ready = sem("k_ready")
        kv_ready = sem("kv_ready")
        roped_cos = sem("roped_cos")
        roped_sin = sem("roped_sin")
        roped = sem("roped")
        q_high = sem("q_high")
        k_high = sem("k_high")
        q_split = sem("q_split")
        k_split = sem("k_split")
        tqk_done = sem("tqk_done")
        tqk_read = sem("tqk_read")
        s_done = sem("s_done")
        s_max = sem("s_max")
        mt_done = sem("mt_done")
        mt_read = sem("mt_read")
        st_done = sem("st_done")
        exp_done = sem("exp_done")
        pv_done = sem("pv_done")
        recip_done = sem("recip_done")
        self_norm = sem("self_norm")
        ot_high = sem("ot_high")
        ot_split = sem("ot_split")
        wo_done = sem("wo_done")
        res_added = sem("res_added")
        stats_done = sem("stats_done")
        mom_done = sem("mom_done")
        eps_done = sem("eps_done")
        rstd_done = sem("rstd_done")
        x1_ready = sem("x1_ready")
        x1t_done = sem("x1t_done")
        x1t_high = sem("x1t_high")
        x1t_split = sem("x1t_split")
        x1_kept = sem("x1_kept")
        xk_done = sem("xk_done")
        xk_copied = sem("xk_copied")
        xq_done = sem("xq_done")
        xq_copied = sem("xq_copied")
        xv_done = sem("xv_done")
        xv_copied = sem("xv_copied")
        xqt_done = sem("xqt_done")
        xqt_high = sem("xqt_high")
        xqt_split = sem("xqt_split")
        xkt_done = sem("xkt_done")
        xkt_high = sem("xkt_high")
        xkt_split = sem("xkt_split")
        sx_done = sem("sx_done")
        sx_max = sem("sx_max")
        mxt_done = sem("mxt_done")
        mxt_read = sem("mxt_read")
        stx_done = sem("stx_done")
        expx_done = sem("expx_done")
        pvx_done = sem("pvx_done")
        xrecip_done = sem("xrecip_done")
        cross_norm = sem("cross_norm")
        oxt_high = sem("oxt_high")
        oxt_split = sem("oxt_split")
        wxo_done = sem("wxo_done")
        yres_added = sem("yres_added")
        ystats_done = sem("ystats_done")
        ymom_done = sem("ymom_done")
        yeps_done = sem("yeps_done")
        yrstd_done = sem("yrstd_done")
        x2_ready = sem("x2_ready")
        moe_loaded = sem("moe_loaded")
        moe_high = sem("moe_high")
        moe_split = sem("moe_split")
        t2_done = sem("t2_done")
        t2_high = sem("t2_high")
        t2_split = sem("t2_split")
        gate_done = sem("gate_done")
        logits_ready = sem("logits_ready")
        top_ready = sem("top_ready")
        top_index = sem("top_index")
        top_step = sem("top_step")
        top_exp = sem("top_exp")
        gates_ready = sem("gates_ready")
        gates_high = sem("gates_high")
        gates_split = sem("gates_split")
        gt_done = sem("gt_done")
        gt_read = sem("gt_read")
        y_done = sem("y_done")
        y_added = sem("y_added")
        ew_high = sem("ew_high")
        ew_split = sem("ew_split")
        fin_stats = sem("fin_stats")
        fin_mom = sem("fin_mom")
        fin_eps = sem("fin_eps")
        fin_rstd = sem("fin_rstd")
        fin_ready = sem("fin_ready")
        w_loaded = {n: sem(f"w_loaded_{n}") for n in ("qkv", "o", "xkv", "xq", "xo")}
        ew_loaded = [sem(f"ew_loaded{i}") for i in range(2)]
        out_stored = [sem(f"out_stored{i}") for i in range(2)]

        banks = ctx.enter_context(nc.psum_tensor("banks", [P, 8, 512], F32))
        PJ = [banks[:, 0, :], banks[:, 1, :]]
        PT = [banks[:, 2, :], banks[:, 3, :]]
        PU = [banks[:, 4, :], banks[:, 5, :]]
        PO = [banks[:, 6, :], banks[:, 7, :]]
        PY = [banks[:, 4 + i, :] for i in range(YB)]

        x2_full = sb("x2", [P, B, D])
        x2 = x2_full[0:T]
        w_landing = x2_full[:].rearrange("p b d -> p (b d)")
        ident = sb("ident", [P, P])
        ident_r = sb("ident_r", [P, P], F32R)
        minus_half = sb("minus_half", [T, 1])
        eps_col = sb("eps_col", [T, 1])

        def three_passes(out, a_hi, a_lo, b_hi, b_lo, first=True, last=True):
            nc.tensor.matmul(out, a_hi, b_hi, start=first, stop=False)
            nc.tensor.matmul(out, a_hi, b_lo, start=False, stop=False)
            return nc.tensor.matmul(out, a_lo, b_hi, start=False, stop=last)

        def project(out, a_hi, a_lo, w_hi, w_lo, cols):
            for k in range(KC):
                mm = three_passes(out, a_hi[:, k, :], a_lo[:, k, :], w_hi[:, k, cols], w_lo[:, k, cols],
                                  k == 0, k == KC - 1)
            return mm

        with ExitStack() as attn:
            def asb(name, shape, dt=F32):
                return sb(name, shape, dt, attn)

            weights = [("qkv", w_qkv, KC, QKVW), ("o", w_o, KC, D), ("xkv", w_xkv, 1, 2 * D),
                       ("xq", w_xq, KC, D), ("xo", w_xo, KC, D)]
            w_order = {name: i for i, (name, *_) in enumerate(weights)}
            w_hi = {n: asb(f"w_{n}_hi", [P, kc, m], F32R) for n, _, kc, m in weights}
            w_lo = {n: asb(f"w_{n}_lo", [P, kc, m], F32R) for n, _, kc, m in weights}
            landing, at = {}, 0
            for n, _, kc, m in weights:
                if at + kc * m > B * D:
                    at = 0
                landing[n] = w_landing[:, at:at + kc * m].rearrange("p (c m) -> p c m", c=kc)
                at += kc * m

            bias_qkv = asb("bias_qkv", [T, QKVW])
            bias_o = asb("bias_o", [T, D])
            cos_t = asb("cos_t", [T, QKW])
            sin_t = asb("sin_t", [T, QKW])
            causal = asb("causal", [T, XC, T], F32R)
            causal_t = asb("causal_t", [T, XC, T], F32R)
            select_in = asb("select_in", [P, 2, T])
            select = asb("select", [P, 2, T], F32R)
            xin = asb("xin", [T, D])
            xres = asb("xres", [T, D])
            xT_in = asb("xT_in", [P, KC, T])
            xT_hi = asb("xT_hi", [P, KC, T], F32R)
            xT_lo = asb("xT_lo", [P, KC, T], F32R)
            qk = asb("qk", [T, QKW])
            rot_c = asb("rot_c", [T, QKW])
            rot_s = asb("rot_s", [T, QKW])
            q_parts = asb("q_parts", [T, HQ, 2, HD], F32R)
            k_parts = asb("k_parts", [T, 2, HKV, 2, HD], F32R)
            qT = asb("qT", [P, 2, J, T], F32R)
            kT = asb("kT", [P, 2, 2, T], F32R)
            v_wide = asb("v_wide", [T, 2, 4, VPITCH])
            row_max = asb("row_max", [T, J, P], F32R)
            maxT = asb("maxT", [P, J * T], F32R)
            probs = asb("probs", [T, 4, J, T])
            causal_in, causal_t_in = probs[:, 0], probs[:, 1]
            recip = asb("recip", [P // 2, J * T])
            summed = rot_s[:, 0:D]
            oT_hi = asb("oT_hi", [P, KC, T], F32R)
            oT_lo = asb("oT_lo", [P, KC, T], F32R)
            stats = asb("stats", [T, 6])
            moments = asb("moments", [T, 2])
            var_eps = asb("var_eps", [T, 1])
            rstd = asb("rstd", [T, 1])
            x1 = asb("x1", [T, D])
            x1_old = asb("x1_old", [T, D])
            cT_in = asb("cT_in", [P, T])
            cT_hi = asb("cT_hi", [P, T], F32R)
            cT_lo = asb("cT_lo", [P, T], F32R)
            x1T_hi = asb("x1T_hi", [P, KC, T], F32R)
            x1T_lo = asb("x1T_lo", [P, KC, T], F32R)
            xq_tok = asb("xq_tok", [T, D])
            xk_oT = asb("xk_oT", [P, D])
            xk_tok = xk_oT[0:T, :]
            oT = xk_oT[:, 0:J * T]
            xv_wide = asb("xv_wide", [T, XH, 2 * XD])
            xqT_hi = asb("xqT_hi", [P, XC, T], F32R)
            xqT_lo = asb("xqT_lo", [P, XC, T], F32R)
            xkT_hi = asb("xkT_hi", [P, XC, T], F32R)
            xkT_lo = asb("xkT_lo", [P, XC, T], F32R)
            xrow_max = asb("xrow_max", [T, XC, P], F32R)
            xmaxT = asb("xmaxT", [P, XC * T], F32R)
            xrecip = asb("xrecip", [P, XC * T])
            oxT = asb("oxT", [P, XC * T])
            summed_y = rot_c[:, 0:D]
            oxT_hi = asb("oxT_hi", [P, KC, T], F32R)
            oxT_lo = asb("oxT_lo", [P, KC, T], F32R)
            ystats = asb("ystats", [T, 6])
            ymoments = asb("ymoments", [T, 2])
            yvar_eps = asb("yvar_eps", [T, 1])
            yrstd = asb("yrstd", [T, 1])

            def chunked(src):
                return src.rearrange("(c p) n -> p c n", p=P)

            def pipeline(eng, step):
                for it in range(3):
                    step(it, True, it >= 1, it >= 2, True)
                with eng.Fori(3, B - 1) as it:
                    step(it, True, True, True, True)
                step(B - 1, True, True, True, False)
                step(B, False, True, True, False)
                step(B + 1, False, False, True, False)

            with nc.Block() as block:

                @block.sync
                def _(sp):
                    def load_weight(n, src):
                        sp.dma_start(landing[n], chunked(src)).then_inc(w_loaded[n], 16)

                    def load_xT(b):
                        sp.wait_ge(x_split, b)
                        sp.dma_start(xT_in[:], xT.rearrange("(c p) (b t) -> b p c t", p=P, t=T)[b])\
                          .then_inc(xT_loaded, 16)

                    def load_xin(b):
                        sp.wait_ge(xres_ready, b)
                        sp.dma_start(xin[:], x[b]).then_inc(xin_loaded, 16)

                    def load_ctx(b):
                        sp.wait_ge(c_split, b)
                        sp.dma_start(cT_in[:], ctxT.rearrange("p (b t) -> b p t", t=T)[b])\
                          .then_inc(ctx_loaded, 16)

                    load_xT(0)
                    load_weight("qkv", w_qkv)
                    for dst, src in ((ident, ident_c), (bias_qkv, b_qkv), (cos_t, rope_cos), (sin_t, rope_sin),
                                     (bias_o, b_o), (select_in, select_c), (causal_in, causal_c), (causal_t_in, causal_t_c)):
                        sp.dma_start(dst[:], src).then_inc(const_loaded, 16)
                    load_xin(0)
                    load_ctx(0)
                    for n, src, _, _ in weights[1:-1]:
                        load_weight(n, src)
                    sp.wait_ge(w_ready, 1)
                    load_weight("xo", w_xo)

                    def step(it, self_, cross, outp, more):
                        if more:
                            load_xT(it + 1)
                            load_xin(it + 1)
                            load_ctx(it + 1)
                    pipeline(sp, step)

                @block.scalar
                def _(act):
                    def copy(dst, src):
                        return nc.scalar.activation(dst, src, ACT.Copy)

                    def split_weight(n):
                        act.wait_ge(w_loaded[n], 16)
                        copy(w_hi[n][:], landing[n]).then_inc(w_high, 1)

                    def split_x(b):
                        act.wait_ge(xT_loaded, 16 * b + 16)
                        act.wait_ge(kv_done, b)
                        copy(xT_hi[:], xT_in[:]).then_inc(x_high, 1)

                    def high_qk(b):
                        act.wait_ge(roped, b + 1)
                        copy(q_parts[:, :, 0, :], qk[:, 0:D].rearrange("t (h d) -> t h d", d=HD))\
                            .then_inc(q_high, 1)
                        for dup in range(2):
                            copy(k_parts[:, 0, :, dup, :], qk[:, D:QKW].rearrange("t (h d) -> t h d", d=HD))\
                                .then_inc(k_high, 1)

                    split_x(0)
                    split_weight("qkv")
                    act.wait_ge(const_loaded, 16 * 8)
                    copy(ident_r[:], ident[:]).then_inc(const_ready, 1)
                    copy(select[:], select_in[:]).then_inc(const_ready, 1)
                    copy(causal[:], causal_in).then_inc(const_ready, 1)
                    copy(causal_t[:], causal_t_in).then_inc(const_ready, 1)
                    high_qk(0)

                    def step(it, self_, cross, outp, more):
                        b, c, y = it, it - 1, it - 2
                        if self_:
                            for n, (dst, bank) in enumerate(((qT[:, 0], PJ[0]), (qT[:, 1], PJ[1]), (kT[:], PO[0]))):
                                act.wait_ge(tqk_done, 3 * b + n + 1)
                                copy(dst, bank[:, 0:4 * T]).then_inc(tqk_read, 1)
                        if cross:
                            act.wait_ge(xk_done, c + 1)
                            copy(xk_tok[:], PU[1][0:T, :]).then_inc(xk_copied, 1)
                            act.wait_ge(xv_done, c + 1)
                            copy(xv_wide[:, :, 0:XD], PJ[1][0:T, :].rearrange("t (h d) -> t h d", d=XD))\
                                .then_inc(xv_copied, 1)
                            act.wait_ge(x1t_done, c + 1)
                            copy(x1T_hi[:], PO[1][:, 0:KC * T]).then_inc(x1t_high, 1)
                        if self_:
                            act.wait_ge(ctx_loaded, 16 * b + 16)
                            copy(cT_hi[:], cT_in[:]).then_inc(c_high, 1)
                        if more:
                            split_x(b + 1)
                        if cross:
                            act.wait_ge(xq_done, c + 1)
                            copy(xq_tok[:], PJ[0][0:T, :]).then_inc(xq_copied, 1)
                        if outp:
                            act.wait_ge(cross_norm, 4 * y + 4)
                            copy(oxT_hi[:], oxT[:]).then_inc(oxt_high, 1)
                        if cross:
                            act.wait_ge(xqt_done, c + 1)
                            copy(xqT_hi[:], PJ[1][:, 0:XC * T]).then_inc(xqt_high, 1)
                            act.wait_ge(xkt_done, c + 1)
                            copy(xkT_hi[:], PO[0][:, 0:XC * T]).then_inc(xkt_high, 1)
                        if self_:
                            act.wait_ge(mt_done, b + 1)
                            copy(maxT[:], PO[1][:, 0:J * T]).then_inc(mt_read, 1)
                        for u in range(HKV):
                            if self_:
                                act.wait_ge(st_done, 8 * b + u + 1)
                                if u >= 4:
                                    act.wait_ge(pv_done, 8 * b + u - 3)
                                elif outp:
                                    act.wait_ge(pvx_done, 4 * it - 7 + u)
                                nc.scalar.activation(probs[:, u % 4], PU[u % 2][0:T, 0:J * T], ACT.Exp,
                                                     scale=SELF_SCALE).then_inc(exp_done, 1)
                            if u == 4 and cross:
                                if outp:
                                    act.wait_ge(yres_added, c)
                                copy(x1_old[:], x1[:]).then_inc(x1_kept, 1)
                        if cross:
                            act.wait_ge(mxt_done, c + 1)
                            copy(xmaxT[:], PJ[1][:, 0:XC * T]).then_inc(mxt_read, 1)
                        if isinstance(it, int) and it == 0:
                            for n in ("o", "xkv", "xq"):
                                split_weight(n)
                        if isinstance(it, int) and it == 1:
                            split_weight("xo")
                        for i in range(XC):
                            if i == XC - 1 and more:
                                high_qk(b + 1)
                            if i == 1 and self_:
                                act.wait_ge(self_norm, 2 * b + 2)
                                copy(oT_hi[:], oT[:]).then_inc(ot_high, 1)
                            if cross:
                                act.wait_ge(stx_done, 4 * c + i + 1)
                                if self_:
                                    act.wait_ge(pv_done, 8 * b + 4 + i + 1)
                                else:
                                    act.wait_ge(pvx_done, 4 * c + i - 3)
                                nc.scalar.activation(probs[:, i], PU[i % 2][0:T, 0:XC * T], ACT.Exp,
                                                     scale=CROSS_SCALE).then_inc(expx_done, 1)
                    pipeline(act, step)

                @block.gpsimd
                def _(pool):
                    def split_x(b):
                        pool.wait_ge(x_high, b + 1)
                        nc.gpsimd.tensor_tensor(xT_lo[:], xT_in[:], xT_hi[:].bitcast(F32), ALU.subtract)\
                            .then_inc(x_split, 1)

                    nc.gpsimd.memset(row_max[:].bitcast(F32), 0.0).then_inc(const_ready, 1)
                    nc.gpsimd.memset(xrow_max[:].bitcast(F32), 0.0).then_inc(const_ready, 1)
                    nc.gpsimd.memset(v_wide[:], 0.0).then_inc(zeroed, 1)
                    pool.wait_ge(zeroed, 1)
                    nc.gpsimd.memset(v_wide[:, :, :, P // 2:P // 2 + HD], 1.0).then_inc(const_ready, 1)
                    nc.gpsimd.memset(xv_wide[:], 1.0).then_inc(const_ready, 1)
                    nc.gpsimd.memset(minus_half[:], -0.5).then_inc(const_ready, 1)
                    nc.gpsimd.memset(eps_col[:], EPS).then_inc(const_ready, 1)
                    def rotate(b, cross_before, outp_before):
                        pool.wait_ge(k_ready, b + 1)
                        if cross_before:
                            pool.wait_ge(roped, b)
                        if outp_before:
                            pool.wait_ge(x2_ready, b - 2)
                        nc.gpsimd.tensor_tensor(rot_c[:], qk[:], cos_t[:], ALU.mult).then_inc(roped_cos, 1)
                        for dup in range(2):
                            pool.wait_ge(k_high, 2 * b + dup + 1)
                            nc.gpsimd.tensor_tensor(k_parts[:, 1, :, dup, :],
                                                    qk[:, D:QKW].rearrange("t (h d) -> t h d", d=HD),
                                                    k_parts[:, 0, :, dup, :].bitcast(F32), ALU.subtract)\
                                .then_inc(k_split, 1)

                    split_x(0)
                    pool.wait_ge(const_loaded, 16 * 8)
                    pool.wait_ge(const_ready, 10)
                    rotate(0, False, False)

                    def step(it, self_, cross, outp, more):
                        b, c, y = it, it - 1, it - 2
                        if cross:
                            pool.wait_ge(mom_done, c + 1)
                            nc.gpsimd.tensor_tensor(var_eps[:], moments[:, 1:2], eps_col[:], ALU.add)\
                                .then_inc(eps_done, 1)
                            pool.wait_ge(eps_done, c + 1)
                            nc.gpsimd.tensor_tensor(rstd[:], var_eps[:], minus_half[:], ALU.pow)\
                                .then_inc(rstd_done, 1)
                        if self_:
                            pool.wait_ge(xin_loaded, 16 * b + 16)
                            pool.wait_ge(res_added, b)
                            nc.gpsimd.tensor_tensor(xres[:], xin[:], bias_o[:], ALU.add).then_inc(xres_ready, 1)
                            pool.wait_ge(c_high, b + 1)
                            nc.gpsimd.tensor_tensor(cT_lo[:], cT_in[:], cT_hi[:].bitcast(F32), ALU.subtract)\
                                .then_inc(c_split, 1)
                        if more:
                            split_x(b + 1)
                        if outp:
                            pool.wait_ge(oxt_high, y + 1)
                            nc.gpsimd.tensor_tensor(oxT_lo[:], oxT[:].rearrange("p (c t) -> p c t", c=KC),
                                                    oxT_hi[:].bitcast(F32), ALU.subtract).then_inc(oxt_split, 1)
                            pool.wait_ge(ymom_done, y + 1)
                            nc.gpsimd.tensor_tensor(yvar_eps[:], ymoments[:, 1:2], eps_col[:], ALU.add)\
                                .then_inc(yeps_done, 1)
                            pool.wait_ge(yeps_done, y + 1)
                            nc.gpsimd.tensor_tensor(yrstd[:], yvar_eps[:], minus_half[:], ALU.pow)\
                                .then_inc(yrstd_done, 1)
                        if more:
                            rotate(b + 1, self_, outp)
                    pipeline(pool, step)

                @block.vector
                def _(dve):
                    v = nc.vector

                    def low_part(dst, src, hi):
                        return v.tensor_tensor(dst, src, hi.bitcast(F32), ALU.subtract)

                    def split_weight(n):
                        dve.wait_ge(w_high, w_order[n] + 1)
                        low_part(w_lo[n][:], landing[n], w_hi[n][:]).then_inc(w_ready, 1)

                    split_weight("qkv")
                    dve.wait_ge(const_ready, 10)
                    dve.wait_ge(const_loaded, 16 * 8)

                    def rotate(b, x1_before):
                        dve.wait_ge(q_done, b + 1)
                        v.tensor_tensor(qk[:, 0:D], PJ[0][0:T, :], bias_qkv[:, 0:D], ALU.add)\
                            .then_inc(q_ready, 1)
                        dve.wait_ge(kv_done, b + 1)
                        v.tensor_tensor(qk[:, D:QKW], PJ[1][0:T, 0:KVW], bias_qkv[:, D:QKW], ALU.add)\
                            .then_inc(k_ready, 1)
                        v.tensor_tensor(v_wide[:, :, :, 0:HD],
                                        PJ[1][0:T, KVW:2 * KVW].rearrange("t (a h d) -> t a h d", a=2, d=HD),
                                        bias_qkv[:, QKW:QKVW].rearrange("t (a h d) -> t a h d", a=2, d=HD),
                                        ALU.add).then_inc(kv_ready, 1)
                        dve.wait_ge(q_ready, b + 1)
                        dve.wait_ge(k_ready, b + 1)
                        if x1_before:
                            dve.wait_ge(x1_ready, b - 1)
                        halves = [t.rearrange("t (h s d) -> t h s d", s=2, d=HD // 2)
                                  for t in (rot_s[:], qk[:], sin_t[:])]
                        for s in range(2):
                            v.tensor_tensor(halves[0][:, :, s], halves[1][:, :, 1 - s], halves[2][:, :, s],
                                            ALU.mult).then_inc(roped_sin, 1)
                        dve.wait_ge(roped_sin, 2 * b + 2)
                        dve.wait_ge(roped_cos, b + 1)
                        v.tensor_tensor(qk[:], rot_c[:], rot_s[:], ALU.add).then_inc(roped, 1)

                    def low_q(b):
                        dve.wait_ge(q_high, b + 1)
                        low_part(q_parts[:, :, 1, :], qk[:, 0:D].rearrange("t (h d) -> t h d", d=HD),
                                 q_parts[:, :, 0, :]).then_inc(q_split, 1)

                    def cross_reciprocals(half, first, last):
                        cols = slice(first * T, last * T)
                        v.reciprocal(xrecip[:, cols], PT[half][:, cols]).then_inc(xrecip_done, 1)

                    def cross_normalise(half):
                        for i in (2 * half, 2 * half + 1):
                            at = 64 * (i % 2)
                            v.tensor_tensor(oxT[XD * i:XD * i + XD, :], PT[half][at:at + XD, 0:XC * T],
                                            xrecip[at + XD:at + 2 * XD, :], ALU.mult).then_inc(cross_norm, 1)

                    rotate(0, False)
                    low_q(0)

                    def step(it, self_, cross, outp, more):
                        b, c, y = it, it - 1, it - 2
                        if cross:
                            dve.wait_ge(wo_done, c + 1)
                            dve.wait_ge(xres_ready, c + 1)
                            if self_:
                                dve.wait_ge(roped, b + 1)
                            v.tensor_tensor(summed[:], PO[1][0:T, :], xres[:], ALU.add).then_inc(res_added, 1)
                            dve.wait_ge(res_added, c + 1)
                            v.bn_stats(stats[:], summed[:]).then_inc(stats_done, 1)
                            dve.wait_ge(const_ready, 10)
                            dve.wait_ge(stats_done, c + 1)
                            v.bn_aggr(moments[:], stats[:]).then_inc(mom_done, 1)
                        if outp:
                            dve.wait_ge(oxt_split, y)
                            dve.wait_ge(xrecip_done, XRECIPS * y + 1)
                            cross_normalise(0)
                        if cross:
                            dve.wait_ge(rstd_done, c + 1)
                            if outp:
                                dve.wait_ge(x1_kept, c)
                            v.tensor_scalar(x1[:], summed[:], moments[:, 0:1], rstd[:], ALU.subtract, ALU.mult)\
                                .then_inc(x1_ready, 1)
                        if outp:
                            dve.wait_ge(pvx_done, 4 * y + 4)
                            dve.wait_ge(cross_norm, 4 * y + 2)
                            cross_reciprocals(1, 0, 1)
                        for g in range(HKV):
                            if g == 1 and cross:
                                dve.wait_ge(x1t_high, c + 1)
                                low_part(x1T_lo[:], PO[1][:, 0:KC * T].rearrange("p (c t) -> p c t", c=KC), x1T_hi[:])\
                                    .then_inc(x1t_split, 1)
                            if self_:
                                dve.wait_ge(s_done, 8 * b + g + 1)
                                col = 32 * (g % 4) + g // 4
                                v.reduce_max(row_max[:, :, col], PU[g % 2][0:T, 0:J * T].rearrange("q (j k) -> q j k", j=J),
                                             AX_X).then_inc(s_max, 1)
                            if 1 <= g < XC and outp:
                                cross_reciprocals(1, g, g + 1)
                            if g == XC and outp:
                                dve.wait_ge(xrecip_done, XRECIPS * y + XRECIPS)
                                cross_normalise(1)
                        if cross:
                            dve.wait_ge(xqt_high, c + 1)
                            low_part(xqT_lo[:], PJ[1][:, 0:XC * T].rearrange("p (c t) -> p c t", c=XC), xqT_hi[:])\
                                .then_inc(xqt_split, 1)
                            dve.wait_ge(xkt_high, c + 1)
                            low_part(xkT_lo[:], PO[0][:, 0:XC * T].rearrange("p (c t) -> p c t", c=XC), xkT_hi[:])\
                                .then_inc(xkt_split, 1)
                        if outp:
                            dve.wait_ge(wxo_done, y + 1)
                            dve.wait_ge(x1_kept, y + 1)
                            v.tensor_tensor(summed_y[:], PT[0][0:T, :], x1_old[:], ALU.add).then_inc(yres_added, 1)
                            dve.wait_ge(yres_added, y + 1)
                            v.bn_stats(ystats[:], summed_y[:]).then_inc(ystats_done, 1)
                            dve.wait_ge(const_ready, 10)
                            dve.wait_ge(ystats_done, y + 1)
                            v.bn_aggr(ymoments[:], ystats[:]).then_inc(ymom_done, 1)
                        for i in range(XC):
                            if cross:
                                dve.wait_ge(sx_done, 4 * c + i + 1)
                                bank = (PJ[0], PT[1])[i % 2]
                                v.reduce_max(xrow_max[:, :, 32 * i], bank[0:T, 0:XC * T].rearrange("q (c k) -> q c k", c=XC),
                                             AX_X).then_inc(sx_max, 1)
                            if i == 1 and outp:
                                dve.wait_ge(yrstd_done, y + 1)
                                v.tensor_scalar(x2[:, y, :], summed_y[:], ymoments[:, 0:1], yrstd[:], ALU.subtract, ALU.mult)\
                                    .then_inc(x2_ready, 1)
                        if self_:
                            for half in range(2):
                                dve.wait_ge(pv_done, 8 * b + 4 * half + 4)
                                dve.wait_ge(self_norm, 2 * b + half)
                                v.reciprocal(recip[:], PO[half][P // 2:P, 0:J * T]).then_inc(recip_done, 1)
                                dve.wait_ge(recip_done, 2 * b + half + 1)
                                v.tensor_tensor(oT[64 * half:64 * half + 64, :], PO[half][0:P // 2, 0:J * T], recip[:],
                                                ALU.mult).then_inc(self_norm, 1)
                        if isinstance(it, int) and it == 0:
                            for n in ("o", "xkv", "xq"):
                                split_weight(n)
                        if isinstance(it, int) and it == 1:
                            split_weight("xo")
                        if self_:
                            dve.wait_ge(ot_high, b + 1)
                            low_part(oT_lo[:], oT[:].rearrange("p (c t) -> p c t", c=KC), oT_hi[:]).then_inc(ot_split, 1)
                        if more:
                            rotate(b + 1, cross)
                        if cross:
                            dve.wait_ge(pvx_done, 4 * c + 2)
                            cross_reciprocals(0, 0, XC)
                        if more:
                            low_q(b + 1)
                    pipeline(dve, step)

                @block.tensor
                def _(pe):
                    mm = nc.tensor.matmul

                    def transposed(bank, tok):
                        for k in range(KC):
                            last = nc.tensor.transpose(bank[:, k * T:(k + 1) * T], tok[:, k * P:(k + 1) * P], ident[0:T, 0:T])
                        return last

                    def project_chunk(out, a_hi, a_lo, n, k, cols=slice(0, D)):
                        return three_passes(out, a_hi[:, k, :], a_lo[:, k, :], w_hi[n][:, k, cols], w_lo[n][:, k, cols],
                                            k == 0, k == KC - 1)

                    def project_qkv(k):
                        last_q = project_chunk(PJ[0][0:T, :], xT_hi, xT_lo, "qkv", k)
                        last_kv = project_chunk(PJ[1][0:T, 0:2 * KVW], xT_hi, xT_lo, "qkv", k, slice(D, QKVW))
                        if k == KC - 1:
                            last_q.then_inc(q_done, 1)
                            last_kv.then_inc(kv_done, 1)

                    pe.wait_ge(const_ready, 10)
                    pe.wait_ge(const_loaded, 16 * 8)
                    pe.wait_ge(w_ready, w_order["qkv"] + 1)
                    pe.wait_ge(x_split, 1)
                    for k in range(KC):
                        project_qkv(k)

                    def step(it, self_, cross, outp, more):
                        b, c, y = it, it - 1, it - 2
                        if self_:
                            pe.wait_ge(q_split, b + 1)
                            pe.wait_ge(kv_ready, b + 1)
                            parts = [q_parts[:].rearrange("t h s d -> t (h s d)")[:, n * P:(n + 1) * P] for n in range(8)]
                            parts += [k_parts[:].rearrange("t s h u d -> t (s h u d)")[:, n * P:(n + 1) * P] for n in range(4)]
                            for n, bank in enumerate((PJ[0], PJ[1], PO[0])):
                                if n == 2:
                                    pe.wait_ge(k_split, 2 * b + 2)
                                for m in range(4):
                                    last = mm(bank[:, m * T:(m + 1) * T], parts[4 * n + m], ident_r[0:T, 0:T],
                                              start=True, stop=True)
                                last.then_inc(tqk_done, 1)
                        if cross:
                            if isinstance(it, int) and it == 1:
                                pe.wait_ge(w_ready, w_order["xkv"] + 1)
                            pe.wait_ge(c_split, c + 1)
                            three_passes(PU[1][0:T, :], cT_hi[:], cT_lo[:], w_hi["xkv"][:, 0, 0:D], w_lo["xkv"][:, 0, 0:D])\
                                .then_inc(xk_done, 1)
                        for g in range(HKV):
                            if g == 1 and cross:
                                if self_:
                                    pe.wait_ge(tqk_read, 3 * b + 2)
                                three_passes(PJ[1][0:T, :], cT_hi[:], cT_lo[:], w_hi["xkv"][:, 0, D:2 * D],
                                             w_lo["xkv"][:, 0, D:2 * D]).then_inc(xv_done, 1)
                                pe.wait_ge(x1_ready, c + 1)
                                transposed(PO[1], x1).then_inc(x1t_done, 1)
                                if isinstance(it, int) and it == 1:
                                    pe.wait_ge(w_ready, w_order["xq"] + 1)
                            if self_:
                                rows, gh = slice(32 * (g % 4), 32 * (g % 4) + 32), g // 4
                                if g == 0:
                                    pe.wait_ge(tqk_read, 3 * b + 3)
                                if g == 1 and cross:
                                    pe.wait_ge(xk_copied, c + 1)
                                if g >= 2:
                                    pe.wait_ge(s_max, 8 * b + g - 1)
                                for j in range(J):
                                    last = mm(PU[g % 2][0:T, j * T:(j + 1) * T], qT[rows, gh, j, :], kT[rows, 0, gh, :],
                                              start=True, stop=True)
                                last.then_inc(s_done, 1)
                            if cross and 1 <= g <= KC:
                                if g == 1:
                                    pe.wait_ge(x1t_split, c + 1)
                                last = project_chunk(PJ[0][0:T, :], x1T_hi, x1T_lo, "xq", g - 1)
                                if g == KC:
                                    last.then_inc(xq_done, 1)
                        if cross:
                            pe.wait_ge(xv_copied, c + 1)
                            pe.wait_ge(xq_copied, c + 1)
                            transposed(PJ[1], xq_tok).then_inc(xqt_done, 1)
                            transposed(PO[0], xk_tok).then_inc(xkt_done, 1)
                        if self_:
                            pe.wait_ge(s_max, 8 * b + 8)
                            for j in range(J):
                                last = mm(PO[1][:, j * T:(j + 1) * T], row_max[:, j, :], ident_r[0:T, 0:T], start=True, stop=True)
                            last.then_inc(mt_done, 1)
                        if outp:
                            if isinstance(it, int) and it == 2:
                                pe.wait_ge(w_ready, w_order["xo"] + 1)
                            pe.wait_ge(oxt_split, y + 1)
                            for k in range(KC):
                                last = project_chunk(PT[0][0:T, :], oxT_hi, oxT_lo, "xo", k)
                            last.then_inc(wxo_done, 1)

                        def cross_scores(i):
                            rows, bank = slice(32 * i, 32 * i + 32), (PJ[0], PT[1])[i % 2]
                            if i >= 2:
                                pe.wait_ge(sx_max, 4 * c + i - 1)
                            mm(bank[0:T, 0:XC * T], ident_r[0:T, 0:T], causal[:], start=True, stop=False)
                            for h in range(XC):
                                last = mm(bank[0:T, h * T:(h + 1) * T], xqT_hi[rows, h, :], xkT_hi[rows, h, :],
                                          start=False, stop=h == XC - 1)
                            last.then_inc(sx_done, 1)

                        def scores_t(g):
                            rows, gh, bank = slice(32 * (g % 4), 32 * (g % 4) + 32), g // 4, PU[g % 2][0:T, 0:J * T]
                            mm(bank, select[rows, gh, :], maxT[rows, :], start=True, stop=False)
                            mm(bank, kT[rows, 0, gh, :], qT[rows, gh], start=False, stop=False)
                            mm(bank, kT[rows, 1, gh, :], qT[rows, gh], start=False, stop=True)\
                                .then_inc(st_done, 1)

                        def values(g):
                            pe.wait_ge(exp_done, 8 * b + g + 1)
                            stationary = v_wide[:, g // 4].rearrange("k h n -> k (h n)")[:, (g % 4) * P:(g % 4 + 1) * P]
                            mm(PO[g // 4][:, 0:J * T], stationary, probs[:, g % 4].rearrange("k j q -> k (j q)"),
                               start=(g % 4 == 0), stop=(g % 4 == 3)).then_inc(pv_done, 1)

                        if self_:
                            pe.wait_ge(mt_read, b + 1)
                            scores_t(0)
                        if cross:
                            pe.wait_ge(xqt_split, c + 1)
                            pe.wait_ge(xkt_split, c + 1)
                        for g in range(1, HKV):
                            if self_:
                                scores_t(g)
                            if cross and g <= XC:
                                cross_scores(g - 1)
                            if self_:
                                values(g - 1)
                        if cross:
                            pe.wait_ge(sx_max, 4 * c + 4)
                            for h in range(XC):
                                last = mm(PJ[1][:, h * T:(h + 1) * T], xrow_max[:, h, :], ident_r[0:T, 0:T], start=True, stop=True)
                            last.then_inc(mxt_done, 1)
                        if self_:
                            values(HKV - 1)
                        if more:
                            pe.wait_ge(x_split, b + 2)
                        if cross:
                            pe.wait_ge(mxt_read, c + 1)
                        for i in range(XC):
                            if cross:
                                rows, bank = slice(32 * i, 32 * i + 32), PU[i % 2][0:T]
                                mm(bank[:, 0:XC * T], ident_r[0:T, 0:T], causal_t[:], start=True, stop=False)
                                mm(bank[:, 0:XC * T], select[rows, 0, :], xmaxT[rows, :], start=False, stop=False)
                                for h in range(XC):
                                    last = three_passes(bank[:, h * T:(h + 1) * T], xkT_hi[rows, h, :], xkT_lo[rows, h, :],
                                                        xqT_hi[rows, h, :], xqT_lo[rows, h, :], False, h == XC - 1)
                                last.then_inc(stx_done, 1)
                            if more and i < 2:
                                project_qkv(2 * i)
                                project_qkv(2 * i + 1)
                            if self_ and i >= 2:
                                if i == 2:
                                    if isinstance(it, int) and it == 0:
                                        pe.wait_ge(w_ready, w_order["o"] + 1)
                                    pe.wait_ge(ot_split, b + 1)
                                for k in (2 * i - 4, 2 * i - 3):
                                    last = project_chunk(PO[1][0:T, :], oT_hi, oT_lo, "o", k)
                                if i == XC - 1:
                                    last.then_inc(wo_done, 1)
                            if cross:
                                pe.wait_ge(expx_done, 4 * c + i + 1)
                                if outp and i == 0:
                                    pe.wait_ge(yres_added, y + 1)
                                for h in range(XC):
                                    last = mm(PT[i // 2][64 * (i % 2):64 * (i % 2) + 64, h * T:(h + 1) * T],
                                              xv_wide[:, XC * i + h, :], probs[:, i, h, :], start=True, stop=True)
                                last.then_inc(pvx_done, 1)
                    pipeline(pe, step)

        x2T_hi = sb("x2T_hi", [P, B, KC, T], F32R)
        x2T_lo = sb("x2T_lo", [P, B, KC, T], F32R)
        ew_in = [sb(f"ew_in{i}", [P, KC, D]) for i in range(2)]
        ew_hi = [sb(f"ew_hi{i}", [P, KC, D], F32R) for i in range(2)]
        ew_lo = [sb(f"ew_lo{i}", [P, KC, D], F32R) for i in range(2)]
        gate_in = sb("gate_in", [P, KC, E])
        gate_hi = sb("gate_hi", [P, KC, E], F32R)
        gate_lo = sb("gate_lo", [P, KC, E], F32R)
        eb_in = sb("eb_in", [2 * E, D])
        eb_hi = sb("eb_hi", [2 * E, D], F32R)
        eb_lo = sb("eb_lo", [2 * E, D], F32R)
        ids = sb("ids", [T, E])
        logits = sb("logits", [T, B, E])
        top = sb("top", [T, B, 8])
        top_at = sb("top_at", [T, B, 8], U32)
        top_atf = sb("top_atf", [T, B, 2])
        diff = sb("diff", [T, B])
        ex = sb("ex", [T, B])
        denom = sb("denom", [T, B])
        share = sb("share", [T, 2, B])
        pick = sb("pick", [T, 2, B, E])
        gates = sb("gates", [T, B, E])
        g_parts = sb("g_parts", [T, B, P], F32R)
        gT = sb("gT", [2 * E, 2, T], F32R)
        fstats = sb("fstats", [T, 2, 6])
        fmoments = sb("fmoments", [T, 2, 2])
        fvar = sb("fvar", [T, 2])
        frstd = sb("frstd", [T, 2])
        fin = sb("fin", [T, 2, D])

        with nc.Block() as block:

            @block.sync
            def _(sp):
                def load_expert(e, slot):
                    sp.dma_start(ew_in[slot][:], w_exp.rearrange("e (c p) n -> e p c n", p=P)[e]).then_inc(ew_loaded[slot], 16)

                load_expert(0, 0)
                sp.dma_start(gate_in[:], w_gate.rearrange("(c p) e -> p c e", p=P)).then_inc(moe_loaded, 16)
                sp.dma_start(eb_in[0:E, :], b_exp).then_inc(moe_loaded, 16)
                sp.dma_start(eb_in[E:2 * E, :], b_exp).then_inc(moe_loaded, 16)
                sp.dma_start(ids[:], expert_ids_c).then_inc(moe_loaded, 16)
                load_expert(1, 1)
                with sp.Fori(1, E // 2) as pair:
                    e = pair * 2
                    for slot in range(2):
                        sp.wait_ge(ew_split, e + slot - 1)
                        load_expert(e + slot, slot)
                for b in range(B):
                    sp.wait_ge(fin_ready, b + 1)
                    sp.dma_start(out[b], fin[:, b % 2, :]).then_inc(out_stored[b % 2], 16)
                sp.wait_ge(out_stored[0], 16 * B // 2)
                sp.wait_ge(out_stored[1], 16 * B // 2)

            @block.scalar
            def _(act):
                def copy(dst, src):
                    return nc.scalar.activation(dst, src, ACT.Copy)

                def high_expert(slot, nth):
                    act.wait_ge(ew_loaded[slot], 16 * nth)
                    copy(ew_hi[slot][:], ew_in[slot][:]).then_inc(ew_high, 1)

                act.wait_ge(moe_loaded, 64)
                copy(gate_hi[:], gate_in[:]).then_inc(moe_high, 1)
                copy(eb_hi[:], eb_in[:]).then_inc(moe_high, 1)
                for b in range(B + 1):
                    if b < B:
                        act.wait_ge(t2_done, b + 1)
                        copy(x2T_hi[:, b], PT[b % 2][:, 0:KC * T]).then_inc(t2_high, 1)
                    if b >= 1:
                        act.wait_ge(gate_done, b)
                        copy(logits[:, b - 1, :], PJ[(b - 1) % 2][0:T, 0:E]).then_inc(logits_ready, 1)
                    if b == 4:
                        high_expert(0, 1)
                    if b == 8:
                        high_expert(1, 1)
                act.wait_ge(top_step, 1)
                nc.scalar.activation(ex[:], diff[:], ACT.Exp).then_inc(top_exp, 1)
                act.wait_ge(gates_ready, 1)
                copy(g_parts[:, :, 0:E], gates[:]).then_inc(gates_high, 1)
                for b in range(B):
                    act.wait_ge(gt_done, b + 1)
                    copy(gT[:, b % 2, :], PT[b % 2][0:2 * E, 0:T]).then_inc(gt_read, 1)
                with act.Fori(1, E // 2) as pair:
                    e = pair * 2
                    for slot in range(2):
                        act.wait_ge(y_done, B * (e + slot))
                        high_expert(slot, pair + 1)

            @block.gpsimd
            def _(pool):
                def low_expert(e, slot):
                    pool.wait_ge(ew_high, e + 1)
                    nc.gpsimd.tensor_tensor(ew_lo[slot][:], ew_in[slot][:], ew_hi[slot][:].bitcast(F32), ALU.subtract)\
                        .then_inc(ew_split, 1)

                nc.gpsimd.memset(g_parts[:].bitcast(F32), 0.0).then_inc(moe_split, 1)
                pool.wait_ge(moe_high, 2)
                nc.gpsimd.tensor_tensor(gate_lo[:], gate_in[:], gate_hi[:].bitcast(F32), ALU.subtract)\
                    .then_inc(moe_split, 1)
                nc.gpsimd.tensor_tensor(eb_lo[:], eb_in[:], eb_hi[:].bitcast(F32), ALU.subtract)\
                    .then_inc(moe_split, 1)
                low_expert(0, 0)
                low_expert(1, 1)
                with pool.Fori(1, E // 2) as pair:
                    e = pair * 2
                    for slot in range(2):
                        low_expert(e + slot, slot)
                for b in range(B):
                    pool.wait_ge(fin_eps, b + 1)
                    nc.gpsimd.tensor_tensor(frstd[:, b % 2:b % 2 + 1], fvar[:, b % 2:b % 2 + 1], minus_half[:], ALU.pow)\
                        .then_inc(fin_rstd, 1)

            @block.vector
            def _(dve):
                v = nc.vector
                for b in range(B + 1):
                    if b < B:
                        dve.wait_ge(t2_high, b + 1)
                        v.tensor_tensor(x2T_lo[:, b], PT[b % 2][:, 0:KC * T].rearrange("p (c t) -> p c t", c=KC),
                                        x2T_hi[:, b].bitcast(F32), ALU.subtract).then_inc(t2_split, 1)
                    if b >= 1:
                        dve.wait_ge(logits_ready, b)
                        v.max(top[:, b - 1, :], logits[:, b - 1, :]).then_inc(top_ready, 1)
                        dve.wait_ge(top_ready, b)
                        v.max_index(top_at[:, b - 1, :], top[:, b - 1, :], logits[:, b - 1, :]).then_inc(top_index, 1)
                v.tensor_tensor(diff[:], top[:, :, 1], top[:, :, 0], ALU.subtract).then_inc(top_step, 1)
                dve.wait_ge(top_index, B)
                v.tensor_copy(top_atf[:], top_at[:, :, 0:2]).then_inc(top_step, 1)
                dve.wait_ge(top_exp, 1)
                v.tensor_scalar(denom[:], ex[:], 1.0, None, ALU.add).then_inc(top_step, 1)
                dve.wait_ge(top_step, 3)
                v.reciprocal(share[:, 0, :], denom[:]).then_inc(top_step, 1)
                dve.wait_ge(top_step, 4)
                v.tensor_tensor(share[:, 1, :], ex[:], share[:, 0, :], ALU.mult).then_inc(top_step, 1)
                dve.wait_ge(moe_loaded, 64)
                for r in range(2):
                    v.tensor_tensor(pick[:, r], ids[:].unsqueeze(1).to_broadcast([T, B, E]),
                                    top_atf[:, :, r].unsqueeze(2).to_broadcast([T, B, E]), ALU.is_equal)\
                        .then_inc(top_step, 1)
                dve.wait_ge(top_step, 7)
                for r in range(2):
                    v.tensor_tensor(pick[:, r], pick[:, r], share[:, r, :].unsqueeze(2).to_broadcast([T, B, E]), ALU.mult)\
                        .then_inc(top_step, 1)
                dve.wait_ge(top_step, 9)
                v.tensor_tensor(gates[:], pick[:, 0], pick[:, 1], ALU.add).then_inc(gates_ready, 1)
                dve.wait_ge(gates_high, 1)
                v.tensor_tensor(g_parts[:, :, E:2 * E], gates[:], g_parts[:, :, 0:E].bitcast(F32), ALU.subtract)\
                    .then_inc(gates_split, 1)
                for b in range(B):
                    dve.wait_ge(y_done, b + 1)
                    v.tensor_tensor(x2[:, b, :], PY[b % YB][0:T, :], x2[:, b, :], ALU.add).then_inc(y_added, 1)

                def add_expert(e, b):
                    dve.wait_ge(y_done, B * e + B + b + 1)
                    dve.wait_ge(y_added, B * e + b + 1)
                    v.scalar_tensor_tensor(out=x2[:, b, :], in0=PY[b % YB][0:T, :], scalar=gates[:, b, bass.ds(e, 1)],
                                           in1=x2[:, b, :], op0=ALU.mult, op1=ALU.add).then_inc(y_added, 1)

                def normalise(b):
                    s = b % 2
                    dve.wait_ge(fin_rstd, b + 1)
                    dve.wait_ge(out_stored[s], 16 * (b // 2))
                    v.tensor_scalar(fin[:, s, :], x2[:, b, :], fmoments[:, s, 0:1], frstd[:, s:s + 1], ALU.subtract, ALU.mult)\
                        .then_inc(fin_ready, 1)

                with dve.Fori(0, E // 2 - 1) as pair:
                    e = pair * 2
                    for slot in range(2):
                        for b in range(B):
                            add_expert(e + slot, b)
                for b in range(B):
                    add_expert(E - 2, b)
                for b in range(B):
                    s = b % 2
                    add_expert(E - 1, b)
                    dve.wait_ge(y_added, B * E + b + 1)
                    v.bn_stats(fstats[:, s, :], x2[:, b, :]).then_inc(fin_stats, 1)
                    dve.wait_ge(fin_stats, b + 1)
                    v.bn_aggr(fmoments[:, s, :], fstats[:, s, :]).then_inc(fin_mom, 1)
                    dve.wait_ge(fin_mom, b + 1)
                    v.tensor_scalar(fvar[:, s:s + 1], fmoments[:, s, 1:2], EPS, None, ALU.add).then_inc(fin_eps, 1)
                    if b >= 1:
                        normalise(b - 1)
                normalise(B - 1)

            @block.tensor
            def _(pe):
                mm = nc.tensor.matmul
                for b in range(B + 1):
                    if b < B:
                        if b >= 2:
                            pe.wait_ge(t2_split, b - 1)
                        for k in range(KC):
                            last = nc.tensor.transpose(PT[b % 2][:, k * T:(k + 1) * T], x2[:, b, k * P:(k + 1) * P], ident[0:T, 0:T])
                        last.then_inc(t2_done, 1)
                    if b == 1:
                        pe.wait_ge(moe_split, 3)
                    if b >= 1:
                        pe.wait_ge(t2_split, b)
                        if b >= 3:
                            pe.wait_ge(logits_ready, b - 2)
                        project(PJ[(b - 1) % 2][0:T, 0:E], x2T_hi[:, b - 1], x2T_lo[:, b - 1], gate_hi, gate_lo, slice(0, E))\
                            .then_inc(gate_done, 1)
                pe.wait_ge(gates_split, 1)
                for b in range(B + 1):
                    if b < B:
                        if b >= 2:
                            pe.wait_ge(gt_read, b - 1)
                        mm(PT[b % 2][:, 0:T], g_parts[:, b, :], ident_r[0:T, 0:T], start=True, stop=True).then_inc(gt_done, 1)
                    if b >= 1:
                        pe.wait_ge(gt_read, b)
                        if b > YB:
                            pe.wait_ge(y_added, b - YB)
                        bank = PY[(b - 1) % YB][0:T, :]
                        mm(bank, gT[:, (b - 1) % 2, :], eb_hi[:], start=True, stop=False)
                        mm(bank, gT[:, (b - 1) % 2, :], eb_lo[:], start=False, stop=True).then_inc(y_done, 1)
                with pe.Fori(0, E // 2) as pair:
                    e = pair * 2
                    for slot in range(2):
                        pe.wait_ge(ew_split, e + slot + 1)
                        for b in range(B):
                            pe.wait_ge(y_added, B * (e + slot) + B + b - YB + 1)
                            project(PY[b % YB][0:T, :], x2T_hi[:, b], x2T_lo[:, b], ew_hi[slot], ew_lo[slot], slice(0, D))\
                                .then_inc(y_done, 1)


def kernel(x, ctx_512, L0_attn_Wq, L0_attn_bq, L0_attn_Wk, L0_attn_bk, L0_attn_Wv, L0_attn_bv, L0_attn_Wo, L0_attn_bo,
           L0_xattn_Wq, L0_xattn_Wkv_expand, L0_xattn_Wout, L0_ffn_gate_w, L0_ffn_expert_w, L0_ffn_expert_b):
    import numpy as np
    import concourse.bacc as bacc
    from concourse.bass_utils import run_bass_kernel_spmd

    def q_order(w):
        return w.reshape(2, 4, J, HD, -1).transpose(0, 2, 1, 3, 4).reshape(D, -1)

    def x_order(w):
        return w.reshape(4, XC, XD, -1).transpose(1, 0, 2, 3).reshape(D, -1)

    def rows(v):
        return np.broadcast_to(np.asarray(v)[None, :], (T, v.shape[0]))

    x, ctx = np.asarray(x), np.asarray(ctx_512)
    wq, bq = q_order(np.asarray(L0_attn_Wq)), q_order(np.asarray(L0_attn_bq)[:, None])[:, 0]
    wkv = np.asarray(L0_xattn_Wkv_expand)
    inv_freq = (1.0 / 10000.0 ** (np.arange(0, HD, 2, dtype=np.float32) / HD)).astype(np.float32)
    ang = np.arange(T, dtype=np.float32)[:, None] * inv_freq[None, :]
    cos, sin = np.cos(ang), np.sin(ang)
    select = np.zeros((P, 2, T), np.float32)
    for strip in range(4):
        for gh in range(2):
            select[32 * strip + gh, gh] = -1.0
    causal = np.where(np.arange(T)[None, :] <= np.arange(T)[:, None], 0.0, -1e30).astype(np.float32)
    arrays = {
        "x": x,
        "xT": x.reshape(B * T, D).T,
        "ctxT": ctx[:, :T, :].reshape(B * T, P).T,
        "w_qkv": np.concatenate([wq, np.asarray(L0_attn_Wk), np.asarray(L0_attn_Wv)]).T,
        "b_qkv": rows(np.concatenate([bq, np.asarray(L0_attn_bk), np.asarray(L0_attn_bv)])),
        "w_o": np.asarray(L0_attn_Wo).T.reshape(HKV, J, HD, D).transpose(1, 0, 2, 3).reshape(D, D),
        "b_o": rows(L0_attn_bo),
        "w_xkv": np.concatenate([x_order(wkv[:D]), wkv[D:]]).T,
        "w_xq": x_order(np.asarray(L0_xattn_Wq)).T,
        "w_xo": x_order(np.asarray(L0_xattn_Wout).T),
        "w_gate": np.asarray(L0_ffn_gate_w).T,
        "w_exp": np.asarray(L0_ffn_expert_w),
        "b_exp": np.asarray(L0_ffn_expert_b),
        "rope_cos": np.tile(np.concatenate([cos, cos], 1), (1, QKW // HD)),
        "rope_sin": np.tile(np.concatenate([-sin, sin], 1), (1, QKW // HD)),
        "ident": np.eye(P, dtype=np.float32),
        "select": select,
        "causal": np.broadcast_to(causal[:, None, :], (T, XC, T)),
        "causal_t": np.broadcast_to(causal.T[:, None, :], (T, XC, T)),
        "expert_ids": np.broadcast_to(np.arange(E, dtype=np.float32)[None, :], (T, E)),
    }
    arrays = {f"in_{k}": np.ascontiguousarray(v) for k, v in arrays.items()}
    nc = bacc.Bacc("TRN2", target_bir_lowering=False, num_devices=1)
    args = [nc.dram_tensor(k, v.shape, mybir.dt.from_np(v.dtype), kind="ExternalInput").ap() for k, v in arrays.items()]
    args.append(nc.dram_tensor("out", (B, T, D), F32, kind="ExternalOutput").ap())
    build_decoder(nc, *args)
    r = run_bass_kernel_spmd(nc, [arrays], core_ids=[0])
    return r.results[0]["out"]
```

```python
from contextlib import ExitStack

import concourse.bass as bass
from concourse import mybir

F32 = mybir.dt.float32
F32R = mybir.dt.float32r
U32 = mybir.dt.uint32
ALU = mybir.AluOpType
ACT = mybir.ActivationFunctionType
AX_X = mybir.AxisListType.X

B, T, D, P = 16, 100, 512, 128
KC = D // P
HQ, HKV, HD = 32, 8, 16
J = HQ // HKV
XH, XD = 16, 32
XC = 4
KVW = HKV * HD
QKW = D + KVW
QKVW = D + 2 * KVW
E = 8
EPS = 1e-5
SELF_SCALE = HD ** -0.5
CROSS_SCALE = XD ** -0.5
VPITCH = P + HD
XRECIPS = 6
GB = 4
NG = B // GB
GT = GB * T
LO = 32


def build_decoder(nc, x, xT, ctxT, w_qkv, b_qkv, w_o, b_o, w_xkv, w_xq, w_xo, w_gate, w_exp, b_exp,
                  rope_cos, rope_sin, ident_c, select_c, causal_c, causal_t_c, expert_ids_c, out):
    with ExitStack() as ctx:
        def sb(name, shape, dt=F32, stack=ctx):
            return stack.enter_context(nc.sbuf_tensor(name, shape, dt))

        def sem(name):
            return ctx.enter_context(nc.semaphore(name))

        const_loaded = sem("const_loaded")
        zeroed = sem("zeroed")
        const_ready = sem("const_ready")
        qkv_high = sem("qkv_high")
        qkv_ready = sem("qkv_ready")
        w_high = sem("w_high")
        w_ready = sem("w_ready")
        xT_loaded = sem("xT_loaded")
        xin_loaded = sem("xin_loaded")
        x_high = sem("x_high")
        x_split = sem("x_split")
        ctx_loaded = sem("ctx_loaded")
        c_high = sem("c_high")
        c_split = sem("c_split")
        xres_ready = sem("xres_ready")
        q_done = sem("q_done")
        kv_done = sem("kv_done")
        q_ready = sem("q_ready")
        k_ready = sem("k_ready")
        kv_ready = sem("kv_ready")
        roped_cos = sem("roped_cos")
        roped_sin = sem("roped_sin")
        roped = sem("roped")
        q_high = sem("q_high")
        k_high = sem("k_high")
        q_split = sem("q_split")
        k_split = sem("k_split")
        kt_done = sem("kt_done")
        qt_done = sem("qt_done")
        kt_read = sem("kt_read")
        qt_read = sem("qt_read")
        s_done = sem("s_done")
        s_max = sem("s_max")
        mt_done = sem("mt_done")
        mt_read = sem("mt_read")
        st_done = sem("st_done")
        exp_done = sem("exp_done")
        pv_done = sem("pv_done")
        recip_done = sem("recip_done")
        self_norm = sem("self_norm")
        ot_high = sem("ot_high")
        ot_split = sem("ot_split")
        wo_done = sem("wo_done")
        res_added = sem("res_added")
        stats_done = sem("stats_done")
        mom_done = sem("mom_done")
        eps_done = sem("eps_done")
        rstd_done = sem("rstd_done")
        x1_ready = sem("x1_ready")
        x1t_done = sem("x1t_done")
        x1t_high = sem("x1t_high")
        x1t_split = sem("x1t_split")
        x1_kept = sem("x1_kept")
        xk_done = sem("xk_done")
        xk_copied = sem("xk_copied")
        xq_done = sem("xq_done")
        xq_copied = sem("xq_copied")
        xv_done = sem("xv_done")
        xv_copied = sem("xv_copied")
        xqt_done = sem("xqt_done")
        xqt_high = sem("xqt_high")
        xqt_split = sem("xqt_split")
        xkt_done = sem("xkt_done")
        xkt_high = sem("xkt_high")
        xkt_split = sem("xkt_split")
        sx_done = sem("sx_done")
        sx_max = sem("sx_max")
        mxt_done = sem("mxt_done")
        mxt_read = sem("mxt_read")
        stx_done = sem("stx_done")
        expx_done = sem("expx_done")
        pvx_done = sem("pvx_done")
        xrecip_done = sem("xrecip_done")
        cross_norm = sem("cross_norm")
        oxt_high = sem("oxt_high")
        oxt_split = sem("oxt_split")
        wxo_done = sem("wxo_done")
        yres_added = sem("yres_added")
        ystats_done = sem("ystats_done")
        ymom_done = sem("ymom_done")
        yeps_done = sem("yeps_done")
        yrstd_done = sem("yrstd_done")
        x2_ready = sem("x2_ready")
        moe_zeroed = sem("moe_zeroed")
        gate_loaded = sem("gate_loaded")
        ids_loaded = sem("ids_loaded")
        eb_loaded = sem("eb_loaded")
        eb_high = sem("eb_high")
        eb_split = sem("eb_split")
        t2_done = sem("t2_done")
        t2_even = sem("t2_even")
        t2_odd = sem("t2_odd")
        gate_done = sem("gate_done")
        logits_ready = sem("logits_ready")
        top_ready = sem("top_ready")
        top_index = sem("top_index")
        top_step = sem("top_step")
        diff_done = sem("diff_done")
        top_exp = sem("top_exp")
        gates_ready = sem("gates_ready")
        gt_done = sem("gt_done")
        gt_high = sem("gt_high")
        gt_split = sem("gt_split")
        gb_done = sem("gb_done")
        scaled = sem("scaled")
        xg_high = sem("xg_high")
        xg_split = sem("xg_split")
        xg_used = sem("xg_used")
        y_done = sem("y_done")
        summed_t = sem("summed_t")
        yt_done = sem("yt_done")
        ew_high = sem("ew_high")
        ew_split = sem("ew_split")
        fin_stats = sem("fin_stats")
        fin_mom = sem("fin_mom")
        fin_eps = sem("fin_eps")
        fin_rstd = sem("fin_rstd")
        fin_ready = sem("fin_ready")
        qkv_loaded = [sem(f"qkv_loaded{k}") for k in range(4)]
        w_loaded = {n: sem(f"w_loaded_{n}") for n in ("o", "xkv", "xq", "xo")}
        ew_loaded = [sem(f"ew_loaded{e}") for e in range(E)]
        fin_free = [sem(f"fin_free{i}") for i in range(GB)]

        banks = ctx.enter_context(nc.psum_tensor("banks", [P, 8, 512], F32))
        PJ = [banks[:, 0, :], banks[:, 1, :]]
        PT = [banks[:, 2, :], banks[:, 3, :]]
        PU = [banks[:, 4, :], banks[:, 5, :]]
        PO = [banks[:, 6, :], banks[:, 7, :]]
        PY = [banks[:, 4 + i, :] for i in range(KC)]
        TB = PY

        with ExitStack() as same_place:
            def room(name, shape, dt=F32):
                return sb(name, shape, dt, same_place)

            pick = room("pick", [T, 2, B, E])
            gT = room("gT", [P, NG, GT], F32R)
            gT_hi, gT_lo = gT[0:E], gT[LO:LO + E]
            spread = room("spread", [P, E], F32R)
            sumT = room("sumT", [P, KC, GT])
            eb_in = sumT[0:E].rearrange("e c n -> e (c n)")[:, 0:D]
            eb_hi = room("eb_hi", [P, D], F32R)
            eb_lo = room("eb_lo", [P, D], F32R)
            fin = room("fin", [T, GB, D])
            with ExitStack() as same_again:
                xg_in1 = sb("xg_in1", [P, KC, GB, T], F32, same_again)
            xg_lo1 = room("xg_lo1", [P, KC, GB, T], F32R)
        x2_full = sb("x2", [P, B, D])
        x2 = x2_full[0:T]
        w_landing = x2_full[:].rearrange("p b d -> p (b d)")
        ident = sb("ident", [P, P])
        ident_r = sb("ident_r", [P, P], F32R)
        minus_half = sb("minus_half", [T, 1])
        eps_col = sb("eps_col", [T, 1])

        def three_passes(out, a_hi, a_lo, b_hi, b_lo, first=True, last=True):
            nc.tensor.matmul(out, a_hi, b_hi, start=first, stop=False)
            nc.tensor.matmul(out, a_hi, b_lo, start=False, stop=False)
            return nc.tensor.matmul(out, a_lo, b_hi, start=False, stop=last)

        with ExitStack() as attn:
            def asb(name, shape, dt=F32):
                return sb(name, shape, dt, attn)

            weights = [("qkv", w_qkv, KC, QKVW), ("o", w_o, KC, D), ("xkv", w_xkv, 1, 2 * D),
                       ("xq", w_xq, KC, D), ("xo", w_xo, KC, D)]
            w_order = {name: i for i, (name, *_) in enumerate(weights[1:])}
            w_hi = {n: asb(f"w_{n}_hi", [P, kc, m], F32R) for n, _, kc, m in weights}
            w_lo = {n: asb(f"w_{n}_lo", [P, kc, m], F32R) for n, _, kc, m in weights}
            landing, at = {}, 0
            for n, _, kc, m in weights:
                if at + kc * m > B * D:
                    at = 0
                landing[n] = w_landing[:, at:at + kc * m].rearrange("p (c m) -> p c m", c=kc)
                at += kc * m

            bias_qkv = asb("bias_qkv", [T, QKVW])
            bias_o = asb("bias_o", [T, D])
            cos_t = asb("cos_t", [T, HD])
            sin_t = asb("sin_t", [T, HD])
            causal = asb("causal", [T, T], F32R)
            causal_t = asb("causal_t", [T, T], F32R)
            select_in = asb("select_in", [P, HKV + XC])
            select = asb("select", [P, HKV + XC], F32R)
            xin = asb("xin", [T, D])
            xres = asb("xres", [T, D])
            xT_in = asb("xT_in", [P, KC, T])
            xT_hi = asb("xT_hi", [P, KC, T], F32R)
            xT_lo = asb("xT_lo", [P, KC, T], F32R)
            qk = asb("qk", [T, QKW])
            rot_c = asb("rot_c", [T, QKW])
            rot_s = asb("rot_s", [T, QKW])
            q_parts = asb("q_parts", [T, HQ, 2, HD], F32R)
            k_parts = asb("k_parts", [T, 2, HKV, 2, HD], F32R)
            qT = asb("qT", [P, 2, J, T], F32R)
            kT = asb("kT", [P, 2, 2, 4, T], F32R)
            v_wide = asb("v_wide", [T, 2, 4, VPITCH])
            row_max = asb("row_max", [T, J, P], F32R)
            maxT = asb("maxT", [P, J * T], F32R)
            probs = asb("probs", [T, 4, J, T])
            causal_in, causal_t_in = probs[:, 0, 0], probs[:, 1, 0]
            summed = rot_s[:, 0:D]
            oT_hi = asb("oT_hi", [P, KC, T], F32R)
            oT_lo = asb("oT_lo", [P, KC, T], F32R)
            norms = asb("norms", [T, 2, 10])
            (stats, moments, var_eps, rstd), (ystats, ymoments, yvar_eps, yrstd) = (
                (norms[:, n, 0:6], norms[:, n, 6:8], norms[:, n, 8:9], norms[:, n, 9:10]) for n in range(2))
            x1 = asb("x1", [T, D])
            x1_old = asb("x1_old", [T, D])
            cT_in = asb("cT_in", [P, T])
            cT_hi = asb("cT_hi", [P, T], F32R)
            cT_lo = asb("cT_lo", [P, T], F32R)
            x1T_hi = asb("x1T_hi", [P, KC, T], F32R)
            x1T_lo = asb("x1T_lo", [P, KC, T], F32R)
            xq_tok = asb("xq_tok", [T, D])
            xk_oT = asb("xk_oT", [P, D])
            xk_tok = xk_oT[0:T, :]
            oT = xk_oT[:, 0:J * T]
            xv_wide = asb("xv_wide", [T, XH, 2 * XD])
            xqT_hi = asb("xqT_hi", [P, XC, 4, T], F32R)
            xqT_lo = asb("xqT_lo", [P, XC, 4, T], F32R)
            xkT_hi = asb("xkT_hi", [P, XC, T], F32R)
            xkT_lo = asb("xkT_lo", [P, XC, T], F32R)
            xrow_max, xmaxT = row_max, maxT
            xrecip = asb("xrecip", [P, XC * T])
            recip = xrecip[0:P // 2, :]
            oxT = asb("oxT", [P, XC * T])
            summed_y = rot_c[:, 0:D]
            oxT_hi = asb("oxT_hi", [P, KC, T], F32R)
            oxT_lo = asb("oxT_lo", [P, KC, T], F32R)

            def chunked(src):
                return src.rearrange("(c p) n -> p c n", p=P)

            def pipeline(eng, step):
                for it in range(3):
                    step(it, True, it >= 1, it >= 2, True)
                with eng.Fori(3, B - 1) as it:
                    step(it, True, True, True, True)
                step(B - 1, True, True, True, False)
                step(B, False, True, True, False)
                step(B + 1, False, False, True, False)

            with nc.Block() as block:

                @block.sync
                def _(sp):
                    def load_weight(n, src):
                        sp.dma_start(landing[n], chunked(src)).then_inc(w_loaded[n], 16)

                    def load_xT(b):
                        sp.wait_ge(x_split, b)
                        sp.dma_start(xT_in[:], xT.rearrange("(c p) (b t) -> b p c t", p=P, t=T)[b])\
                          .then_inc(xT_loaded, 16)

                    def load_xin(b):
                        sp.wait_ge(xres_ready, b)
                        sp.dma_start(xin[:], x[b]).then_inc(xin_loaded, 16)

                    def load_ctx(b):
                        sp.wait_ge(c_split, b)
                        sp.dma_start(cT_in[:], ctxT.rearrange("p (b t) -> b p t", t=T)[b])\
                          .then_inc(ctx_loaded, 16)

                    load_xT(0)
                    for k in range(KC):
                        sp.dma_start(landing["qkv"][:, k], chunked(w_qkv)[:, k]).then_inc(qkv_loaded[k], 16)
                    for dst, src in ((ident, ident_c), (bias_qkv, b_qkv), (cos_t, rope_cos), (sin_t, rope_sin),
                                     (bias_o, b_o), (select_in, select_c), (causal_in, causal_c), (causal_t_in, causal_t_c)):
                        sp.dma_start(dst[:], src).then_inc(const_loaded, 16)
                    load_xin(0)
                    load_ctx(0)
                    for n, src, _, _ in weights[1:-1]:
                        load_weight(n, src)
                    sp.wait_ge(qkv_ready, KC)
                    load_weight("xo", w_xo)

                    def step(it, self_, cross, outp, more):
                        if more:
                            load_xT(it + 1)
                            load_xin(it + 1)
                            load_ctx(it + 1)
                    pipeline(sp, step)

                @block.scalar
                def _(act):
                    def copy(dst, src):
                        return nc.scalar.activation(dst, src, ACT.Copy)

                    def split_weight(n):
                        act.wait_ge(w_loaded[n], 16)
                        copy(w_hi[n][:], landing[n]).then_inc(w_high, 1)

                    def split_x(b):
                        act.wait_ge(xT_loaded, 16 * b + 16)
                        act.wait_ge(kv_done, b)
                        copy(xT_hi[:], xT_in[:]).then_inc(x_high, 1)

                    def copy_kT(b):
                        act.wait_ge(kt_done, b + 1)
                        for strip in range(4):
                            rows = slice(32 * strip, 32 * strip + 32)
                            copy(kT[rows, :, :, strip, :], PO[0][rows, 0:4 * T].rearrange("p (s h t) -> p s h t", s=2, h=2))\
                                .then_inc(kt_read, 1)

                    def high_qk(b):
                        act.wait_ge(roped, b + 1)
                        copy(q_parts[:, :, 0, :], qk[:, 0:D].rearrange("t (h d) -> t h d", d=HD))\
                            .then_inc(q_high, 1)
                        for dup in range(2):
                            copy(k_parts[:, 0, :, dup, :], qk[:, D:QKW].rearrange("t (h d) -> t h d", d=HD))\
                                .then_inc(k_high, 1)

                    split_x(0)
                    for k in range(KC):
                        act.wait_ge(qkv_loaded[k], 16)
                        copy(w_hi["qkv"][:, k], landing["qkv"][:, k]).then_inc(qkv_high, 1)
                    act.wait_ge(const_loaded, 16 * 8)
                    copy(ident_r[:], ident[:]).then_inc(const_ready, 1)
                    copy(select[:], select_in[:]).then_inc(const_ready, 1)
                    copy(causal[:], causal_in).then_inc(const_ready, 1)
                    copy(causal_t[:], causal_t_in).then_inc(const_ready, 1)
                    high_qk(0)
                    act.wait_ge(const_ready, 12)
                    copy_kT(0)

                    def step(it, self_, cross, outp, more):
                        b, c, y = it, it - 1, it - 2
                        if self_:
                            for n in range(2):
                                act.wait_ge(qt_done, 2 * b + n + 1)
                                copy(qT[:, n], PJ[n][:, 0:4 * T]).then_inc(qt_read, 1)
                        if cross:
                            act.wait_ge(x1t_done, c + 1)
                            copy(x1T_hi[:], PO[1][:, 0:KC * T]).then_inc(x1t_high, 1)
                            act.wait_ge(xk_done, c + 1)
                            copy(xk_tok[:], PU[1][0:T, :]).then_inc(xk_copied, 1)
                            act.wait_ge(xv_done, c + 1)
                            copy(xv_wide[:, :, 0:XD], PJ[1][0:T, :].rearrange("t (h d) -> t h d", d=XD))\
                                .then_inc(xv_copied, 1)
                        if self_:
                            act.wait_ge(ctx_loaded, 16 * b + 16)
                            copy(cT_hi[:], cT_in[:]).then_inc(c_high, 1)
                        if isinstance(it, int) and it == 0:
                            for n in ("o", "xkv", "xq"):
                                split_weight(n)
                        if more:
                            split_x(b + 1)
                        if cross:
                            act.wait_ge(xq_done, c + 1)
                            copy(xq_tok[:], PJ[0][0:T, :]).then_inc(xq_copied, 1)
                        if outp:
                            act.wait_ge(cross_norm, 4 * y + 4)
                            copy(oxT_hi[:], oxT[:]).then_inc(oxt_high, 1)
                        if cross:
                            act.wait_ge(xqt_done, c + 1)
                            for strip in range(4):
                                rows = slice(32 * strip, 32 * strip + 32)
                                copy(xqT_hi[rows, :, strip, :], PJ[1][rows, 0:XC * T].rearrange("p (c t) -> p c t", c=XC))\
                                    .then_inc(xqt_high, 1)
                            act.wait_ge(xkt_done, c + 1)
                            copy(xkT_hi[:], PO[0][:, 0:XC * T]).then_inc(xkt_high, 1)
                        if self_:
                            act.wait_ge(mt_done, b + 1)
                            copy(maxT[:], PO[1][:, 0:J * T]).then_inc(mt_read, 1)
                        for u in range(HKV):
                            if self_:
                                act.wait_ge(st_done, 8 * b + u + 1)
                                if u >= 4:
                                    act.wait_ge(pv_done, 8 * b + u - 3)
                                elif outp:
                                    act.wait_ge(pvx_done, 4 * it - 7 + u)
                                nc.scalar.activation(probs[:, u % 4], PU[u % 2][0:T, 0:J * T], ACT.Exp,
                                                     scale=SELF_SCALE).then_inc(exp_done, 1)
                            if u == 4 and cross:
                                if outp:
                                    act.wait_ge(yres_added, c)
                                copy(x1_old[:], x1[:]).then_inc(x1_kept, 1)
                        if cross:
                            act.wait_ge(mxt_done, c + 1)
                            copy(xmaxT[:], PJ[1][:, 0:XC * T]).then_inc(mxt_read, 1)
                        if isinstance(it, int) and it == 1:
                            split_weight("xo")
                        for i in range(XC):
                            if i == 2 and more:
                                high_qk(b + 1)
                            if i == 1 and self_:
                                act.wait_ge(self_norm, 2 * b + 2)
                                copy(oT_hi[:], oT[:]).then_inc(ot_high, 1)
                            if cross:
                                act.wait_ge(stx_done, 4 * c + i + 1)
                                if self_:
                                    act.wait_ge(pv_done, 8 * b + 4 + i + 1)
                                else:
                                    act.wait_ge(pvx_done, 4 * c + i - 3)
                                nc.scalar.activation(probs[:, i], PU[i % 2][0:T, 0:XC * T], ACT.Exp,
                                                     scale=CROSS_SCALE).then_inc(expx_done, 1)
                        if more:
                            copy_kT(b + 1)
                    pipeline(act, step)

                @block.gpsimd
                def _(pool):
                    def split_x(b):
                        pool.wait_ge(x_high, b + 1)
                        nc.gpsimd.tensor_tensor(xT_lo[:], xT_in[:], xT_hi[:].bitcast(F32), ALU.subtract)\
                            .then_inc(x_split, 1)

                    nc.gpsimd.memset(row_max[:].bitcast(F32), 0.0).then_inc(const_ready, 1)
                    nc.gpsimd.memset(xqT_hi[:].bitcast(F32), 0.0).then_inc(const_ready, 1)
                    nc.gpsimd.memset(xqT_lo[:].bitcast(F32), 0.0).then_inc(const_ready, 1)
                    split_x(0)
                    nc.gpsimd.memset(v_wide[:], 0.0).then_inc(zeroed, 1)
                    pool.wait_ge(zeroed, 1)
                    nc.gpsimd.memset(v_wide[:, :, :, P // 2:P // 2 + HD], 1.0).then_inc(const_ready, 1)
                    nc.gpsimd.memset(xv_wide[:], 1.0).then_inc(const_ready, 1)
                    nc.gpsimd.memset(kT[:].bitcast(F32), 0.0).then_inc(const_ready, 1)
                    nc.gpsimd.memset(minus_half[:], -0.5).then_inc(const_ready, 1)
                    nc.gpsimd.memset(eps_col[:], EPS).then_inc(const_ready, 1)

                    def rotate(b, cross_before, outp_before):
                        pool.wait_ge(k_ready, b + 1)
                        if cross_before:
                            pool.wait_ge(roped, b)
                        if outp_before:
                            pool.wait_ge(x2_ready, b - 2)
                        nc.gpsimd.tensor_tensor(rot_c[:].rearrange("t (h d) -> t h d", d=HD), qk[:].rearrange("t (h d) -> t h d", d=HD),
                                                cos_t[:].unsqueeze(1).to_broadcast([T, HQ + HKV, HD]), ALU.mult)\
                            .then_inc(roped_cos, 1)
                        for dup in range(2):
                            pool.wait_ge(k_high, 2 * b + dup + 1)
                            nc.gpsimd.tensor_tensor(k_parts[:, 1, :, dup, :],
                                                    qk[:, D:QKW].rearrange("t (h d) -> t h d", d=HD),
                                                    k_parts[:, 0, :, dup, :].bitcast(F32), ALU.subtract)\
                                .then_inc(k_split, 1)

                    pool.wait_ge(const_loaded, 16 * 8)
                    pool.wait_ge(const_ready, 12)
                    rotate(0, False, False)

                    def step(it, self_, cross, outp, more):
                        b, c, y = it, it - 1, it - 2
                        if self_:
                            pool.wait_ge(xin_loaded, 16 * b + 16)
                            pool.wait_ge(res_added, b)
                            nc.gpsimd.tensor_tensor(xres[:], xin[:], bias_o[:], ALU.add).then_inc(xres_ready, 1)
                            pool.wait_ge(c_high, b + 1)
                            nc.gpsimd.tensor_tensor(cT_lo[:], cT_in[:], cT_hi[:].bitcast(F32), ALU.subtract)\
                                .then_inc(c_split, 1)
                        if more:
                            split_x(b + 1)
                        if outp:
                            pool.wait_ge(oxt_high, y + 1)
                            nc.gpsimd.tensor_tensor(oxT_lo[:], oxT[:].rearrange("p (c t) -> p c t", c=KC),
                                                    oxT_hi[:].bitcast(F32), ALU.subtract).then_inc(oxt_split, 1)
                            pool.wait_ge(ymom_done, y + 1)
                            nc.gpsimd.tensor_tensor(yvar_eps[:], ymoments[:, 1:2], eps_col[:], ALU.add)\
                                .then_inc(yeps_done, 1)
                            pool.wait_ge(yeps_done, y + 1)
                            nc.gpsimd.tensor_tensor(yrstd[:], yvar_eps[:], minus_half[:], ALU.pow)\
                                .then_inc(yrstd_done, 1)
                        if more:
                            rotate(b + 1, self_, outp)
                        if self_:
                            pool.wait_ge(mom_done, b + 1)
                            nc.gpsimd.tensor_tensor(var_eps[:], moments[:, 1:2], eps_col[:], ALU.add)\
                                .then_inc(eps_done, 1)
                            pool.wait_ge(eps_done, b + 1)
                            nc.gpsimd.tensor_tensor(rstd[:], var_eps[:], minus_half[:], ALU.pow)\
                                .then_inc(rstd_done, 1)
                    pipeline(pool, step)

                @block.vector
                def _(dve):
                    v = nc.vector

                    def low_part(dst, src, hi):
                        return v.tensor_tensor(dst, src, hi.bitcast(F32), ALU.subtract)

                    def split_weight(n):
                        dve.wait_ge(w_high, w_order[n] + 1)
                        low_part(w_lo[n][:], landing[n], w_hi[n][:]).then_inc(w_ready, 1)

                    for k in range(KC):
                        dve.wait_ge(qkv_high, k + 1)
                        low_part(w_lo["qkv"][:, k], landing["qkv"][:, k], w_hi["qkv"][:, k]).then_inc(qkv_ready, 1)
                    dve.wait_ge(const_ready, 12)
                    dve.wait_ge(const_loaded, 16 * 8)

                    def rotate(b, x1_before):
                        dve.wait_ge(q_done, b + 1)
                        v.tensor_tensor(qk[:, 0:D], PJ[0][0:T, :], bias_qkv[:, 0:D], ALU.add)\
                            .then_inc(q_ready, 1)
                        dve.wait_ge(kv_done, b + 1)
                        v.tensor_tensor(qk[:, D:QKW], PJ[1][0:T, 0:KVW], bias_qkv[:, D:QKW], ALU.add)\
                            .then_inc(k_ready, 1)
                        v.tensor_tensor(v_wide[:, :, :, 0:HD],
                                        PJ[1][0:T, KVW:2 * KVW].rearrange("t (a h d) -> t a h d", a=2, d=HD),
                                        bias_qkv[:, QKW:QKVW].rearrange("t (a h d) -> t a h d", a=2, d=HD),
                                        ALU.add).then_inc(kv_ready, 1)
                        dve.wait_ge(q_ready, b + 1)
                        dve.wait_ge(k_ready, b + 1)
                        if x1_before:
                            dve.wait_ge(x1_ready, b - 1)
                        halves = [t.rearrange("t (h s d) -> t h s d", s=2, d=HD // 2) for t in (rot_s[:], qk[:])]
                        for s in range(2):
                            sines = sin_t[:, s * HD // 2:(s + 1) * HD // 2].unsqueeze(1).to_broadcast([T, HQ + HKV, HD // 2])
                            v.tensor_tensor(halves[0][:, :, s], halves[1][:, :, 1 - s], sines,
                                            ALU.mult).then_inc(roped_sin, 1)
                        dve.wait_ge(roped_sin, 2 * b + 2)
                        dve.wait_ge(roped_cos, b + 1)
                        v.tensor_tensor(qk[:], rot_c[:], rot_s[:], ALU.add).then_inc(roped, 1)

                    def low_q(b):
                        dve.wait_ge(q_high, b + 1)
                        low_part(q_parts[:, :, 1, :], qk[:, 0:D].rearrange("t (h d) -> t h d", d=HD),
                                 q_parts[:, :, 0, :]).then_inc(q_split, 1)

                    def cross_reciprocals(half, first, last):
                        cols = slice(first * T, last * T)
                        v.reciprocal(xrecip[:, cols], PT[half][:, cols]).then_inc(xrecip_done, 1)

                    def cross_normalise(i):
                        at = 64 * (i % 2)
                        v.tensor_tensor(oxT[XD * i:XD * i + XD, :], PT[i // 2][at:at + XD, 0:XC * T],
                                        xrecip[at + XD:at + 2 * XD, :], ALU.mult).then_inc(cross_norm, 1)

                    rotate(0, False)
                    low_q(0)

                    def step(it, self_, cross, outp, more):
                        b, c, y = it, it - 1, it - 2
                        if outp:
                            dve.wait_ge(pvx_done, 4 * y + 4)
                            dve.wait_ge(cross_norm, 4 * y + 2)
                            cross_reciprocals(1, 0, 1)
                        for g in range(HKV):
                            if g == 0 and cross:
                                dve.wait_ge(x1t_high, c + 1)
                                low_part(x1T_lo[:], PO[1][:, 0:KC * T].rearrange("p (c t) -> p c t", c=KC), x1T_hi[:])\
                                    .then_inc(x1t_split, 1)
                            if self_:
                                dve.wait_ge(s_done, 8 * b + g + 1)
                                col = 32 * (g % 4) + g // 4
                                v.reduce_max(row_max[:, :, col], PU[g % 2][0:T, 0:J * T].rearrange("q (j k) -> q j k", j=J),
                                             AX_X).then_inc(s_max, 1)
                            if g == 0 and outp:
                                cross_reciprocals(1, 1, 3)
                            if g == 1 and outp:
                                cross_reciprocals(1, 3, 4)
                            if g == 2 and outp:
                                dve.wait_ge(xrecip_done, XRECIPS * y + XRECIPS)
                                cross_normalise(2)
                            if g == 3 and outp:
                                cross_normalise(3)
                        if isinstance(it, int) and it == 0:
                            for n in ("o", "xkv", "xq"):
                                split_weight(n)
                        if cross:
                            for strip in range(4):
                                rows = slice(32 * strip, 32 * strip + 32)
                                dve.wait_ge(xqt_high, 4 * c + strip + 1)
                                low_part(xqT_lo[rows, :, strip, :], PJ[1][rows, 0:XC * T].rearrange("p (c t) -> p c t", c=XC),
                                         xqT_hi[rows, :, strip, :]).then_inc(xqt_split, 1)
                            dve.wait_ge(xkt_high, c + 1)
                            low_part(xkT_lo[:], PO[0][:, 0:XC * T].rearrange("p (c t) -> p c t", c=XC), xkT_hi[:])\
                                .then_inc(xkt_split, 1)
                        if outp:
                            dve.wait_ge(wxo_done, y + 1)
                            dve.wait_ge(x1_kept, y + 1)
                            v.tensor_tensor(summed_y[:], PT[0][0:T, :], x1_old[:], ALU.add).then_inc(yres_added, 1)
                            dve.wait_ge(yres_added, y + 1)
                            v.bn_stats(ystats[:], summed_y[:]).then_inc(ystats_done, 1)
                            dve.wait_ge(const_ready, 12)
                            dve.wait_ge(ystats_done, y + 1)
                            v.bn_aggr(ymoments[:], ystats[:]).then_inc(ymom_done, 1)
                        for i in range(XC):
                            if cross:
                                dve.wait_ge(sx_done, 4 * c + i + 1)
                                bank = (PJ[0], PT[1])[i % 2]
                                v.reduce_max(xrow_max[:, i].rearrange("q (h r) -> q h r", h=XC)[:, :, 2], bank[0:T, 0:XC * T].rearrange("q (c k) -> q c k", c=XC),
                                             AX_X).then_inc(sx_max, 1)
                            if i == 1 and outp:
                                dve.wait_ge(yrstd_done, y + 1)
                                v.tensor_scalar(x2[:, y, :], summed_y[:], ymoments[:, 0:1], yrstd[:], ALU.subtract, ALU.mult)\
                                    .then_inc(x2_ready, 1)
                        if self_:
                            for half in range(2):
                                dve.wait_ge(pv_done, 8 * b + 4 * half + 4)
                                dve.wait_ge(self_norm, 2 * b + half)
                                if outp and half == 0:
                                    dve.wait_ge(cross_norm, 4 * y + 4)
                                v.reciprocal(recip[:], PO[half][P // 2:P, 0:J * T]).then_inc(recip_done, 1)
                                dve.wait_ge(recip_done, 2 * b + half + 1)
                                v.tensor_tensor(oT[64 * half:64 * half + 64, :], PO[half][0:P // 2, 0:J * T], recip[:],
                                                ALU.mult).then_inc(self_norm, 1)
                        if isinstance(it, int) and it == 1:
                            split_weight("xo")
                        if self_:
                            dve.wait_ge(ot_high, b + 1)
                            low_part(oT_lo[:], oT[:].rearrange("p (c t) -> p c t", c=KC), oT_hi[:]).then_inc(ot_split, 1)
                        if more:
                            rotate(b + 1, cross)
                        if cross:
                            dve.wait_ge(pvx_done, 4 * c + 2)
                            if self_:
                                dve.wait_ge(self_norm, 2 * b + 2)
                            cross_reciprocals(0, 0, 1)
                        if more:
                            low_q(b + 1)
                        if cross:
                            cross_reciprocals(0, 1, 3)
                        if self_:
                            dve.wait_ge(wo_done, b + 1)
                            dve.wait_ge(xres_ready, b + 1)
                            if more:
                                dve.wait_ge(roped, b + 2)
                            v.tensor_tensor(summed[:], PO[1][0:T, :], xres[:], ALU.add).then_inc(res_added, 1)
                            dve.wait_ge(res_added, b + 1)
                            v.bn_stats(stats[:], summed[:]).then_inc(stats_done, 1)
                            dve.wait_ge(const_ready, 12)
                            dve.wait_ge(stats_done, b + 1)
                            v.bn_aggr(moments[:], stats[:]).then_inc(mom_done, 1)
                        if cross:
                            cross_reciprocals(0, 3, 4)
                        if self_:
                            dve.wait_ge(rstd_done, b + 1)
                            if cross:
                                dve.wait_ge(x1_kept, b)
                            v.tensor_scalar(x1[:], summed[:], moments[:, 0:1], rstd[:], ALU.subtract, ALU.mult)\
                                .then_inc(x1_ready, 1)
                        if cross:
                            if outp:
                                dve.wait_ge(oxt_split, c)
                            dve.wait_ge(xrecip_done, XRECIPS * c + 3)
                            cross_normalise(0)
                            cross_normalise(1)
                    pipeline(dve, step)

                @block.tensor
                def _(pe):
                    mm = nc.tensor.matmul

                    def transposed(bank, tok):
                        for k in range(KC):
                            last = nc.tensor.transpose(bank[:, k * T:(k + 1) * T], tok[:, k * P:(k + 1) * P], ident[0:T, 0:T])
                        return last

                    def project_chunk(out, a_hi, a_lo, n, k, cols=slice(0, D)):
                        return three_passes(out, a_hi[:, k, :], a_lo[:, k, :], w_hi[n][:, k, cols], w_lo[n][:, k, cols],
                                            k == 0, k == KC - 1)

                    def project_qkv(k):
                        last_q = project_chunk(PJ[0][0:T, :], xT_hi, xT_lo, "qkv", k)
                        last_kv = project_chunk(PJ[1][0:T, 0:2 * KVW], xT_hi, xT_lo, "qkv", k, slice(D, QKVW))
                        if k == KC - 1:
                            last_q.then_inc(q_done, 1)
                            last_kv.then_inc(kv_done, 1)

                    def transpose_k(b):
                        pe.wait_ge(k_split, 2 * b + 2)
                        parts = k_parts[:].rearrange("t s h u d -> t (s h u d)")
                        for m in range(4):
                            last = mm(PO[0][:, m * T:(m + 1) * T], parts[:, m * P:(m + 1) * P], ident_r[0:T, 0:T],
                                      start=True, stop=True)
                        last.then_inc(kt_done, 1)

                    pe.wait_ge(x_split, 1)
                    for k in range(KC):
                        pe.wait_ge(qkv_ready, k + 1)
                        project_qkv(k)
                    pe.wait_ge(const_ready, 12)
                    pe.wait_ge(const_loaded, 16 * 8)
                    transpose_k(0)

                    def step(it, self_, cross, outp, more):
                        b, c, y = it, it - 1, it - 2
                        if self_:
                            pe.wait_ge(q_split, b + 1)
                            pe.wait_ge(kv_ready, b + 1)
                            parts = q_parts[:].rearrange("t h s d -> t (h s d)")
                            for n in range(2):
                                for m in range(4):
                                    last = mm(PJ[n][:, m * T:(m + 1) * T], parts[:, (4 * n + m) * P:(4 * n + m + 1) * P],
                                              ident_r[0:T, 0:T], start=True, stop=True)
                                last.then_inc(qt_done, 1)
                        if cross:
                            pe.wait_ge(x1_ready, c + 1)
                            transposed(PO[1], x1).then_inc(x1t_done, 1)
                            if isinstance(it, int) and it == 1:
                                pe.wait_ge(w_ready, w_order["xkv"] + 1)
                            pe.wait_ge(c_split, c + 1)
                            three_passes(PU[1][0:T, :], cT_hi[:], cT_lo[:], w_hi["xkv"][:, 0, 0:D], w_lo["xkv"][:, 0, 0:D])\
                                .then_inc(xk_done, 1)
                        for g in range(HKV):
                            if g == 1 and cross:
                                if self_:
                                    pe.wait_ge(qt_read, 2 * b + 2)
                                three_passes(PJ[1][0:T, :], cT_hi[:], cT_lo[:], w_hi["xkv"][:, 0, D:2 * D],
                                             w_lo["xkv"][:, 0, D:2 * D]).then_inc(xv_done, 1)
                                if isinstance(it, int) and it == 1:
                                    pe.wait_ge(w_ready, w_order["xq"] + 1)
                            if self_:
                                gh = g // 4
                                if g == 0:
                                    pe.wait_ge(kt_read, 4 * b + 4)
                                    pe.wait_ge(qt_read, 2 * b + 2)
                                if g == 1 and cross:
                                    pe.wait_ge(xk_copied, c + 1)
                                if g >= 2:
                                    pe.wait_ge(s_max, 8 * b + g - 1)
                                for j in range(J):
                                    last = mm(PU[g % 2][0:T, j * T:(j + 1) * T], qT[:, gh, j, :], kT[:, 0, gh, g % 4, :],
                                              start=True, stop=True)
                                last.then_inc(s_done, 1)
                            if cross and 1 <= g <= KC:
                                if g == 1:
                                    pe.wait_ge(x1t_split, c + 1)
                                last = project_chunk(PJ[0][0:T, :], x1T_hi, x1T_lo, "xq", g - 1)
                                if g == KC:
                                    last.then_inc(xq_done, 1)
                        if cross:
                            pe.wait_ge(xv_copied, c + 1)
                            pe.wait_ge(xq_copied, c + 1)
                            transposed(PJ[1], xq_tok).then_inc(xqt_done, 1)
                            transposed(PO[0], xk_tok).then_inc(xkt_done, 1)
                        if self_:
                            pe.wait_ge(s_max, 8 * b + 8)
                            for j in range(J):
                                last = mm(PO[1][:, j * T:(j + 1) * T], row_max[:, j, :], ident_r[0:T, 0:T], start=True, stop=True)
                            last.then_inc(mt_done, 1)
                        if outp:
                            if isinstance(it, int) and it == 2:
                                pe.wait_ge(w_ready, w_order["xo"] + 1)
                            pe.wait_ge(oxt_split, y + 1)
                            for k in range(KC):
                                last = project_chunk(PT[0][0:T, :], oxT_hi, oxT_lo, "xo", k)
                            last.then_inc(wxo_done, 1)

                        def cross_scores(i):
                            bank = (PJ[0], PT[1])[i % 2]
                            if i >= 2:
                                pe.wait_ge(sx_max, 4 * c + i - 1)
                            mm(bank[0:T, 0:XC * T].rearrange("q (h k) -> q h k", h=XC), ident_r[0:T, 0:T],
                               causal[:].unsqueeze(1).to_broadcast([T, XC, T]), start=True, stop=False)
                            for h in range(XC):
                                last = mm(bank[0:T, h * T:(h + 1) * T], xqT_hi[:, h, i, :], xkT_hi[:, h, :],
                                          start=False, stop=h == XC - 1)
                            last.then_inc(sx_done, 1)

                        def scores_t(g):
                            gh, bank = g // 4, PU[g % 2][0:T, 0:J * T]
                            mm(bank, select[:, g:g + 1].to_broadcast([P, T]), maxT[:], start=True, stop=False)
                            mm(bank, kT[:, 0, gh, g % 4, :], qT[:, gh], start=False, stop=False)
                            mm(bank, kT[:, 1, gh, g % 4, :], qT[:, gh], start=False, stop=True)\
                                .then_inc(st_done, 1)

                        def values(g):
                            pe.wait_ge(exp_done, 8 * b + g + 1)
                            stationary = v_wide[:, g // 4].rearrange("k h n -> k (h n)")[:, (g % 4) * P:(g % 4 + 1) * P]
                            mm(PO[g // 4][:, 0:J * T], stationary, probs[:, g % 4].rearrange("k j q -> k (j q)"),
                               start=(g % 4 == 0), stop=(g % 4 == 3)).then_inc(pv_done, 1)

                        if self_:
                            pe.wait_ge(mt_read, b + 1)
                            scores_t(0)
                        if cross:
                            pe.wait_ge(xqt_split, 4 * c + 4)
                            pe.wait_ge(xkt_split, c + 1)
                        for g in range(1, HKV):
                            if self_:
                                scores_t(g)
                            if cross and g <= XC:
                                cross_scores(g - 1)
                            if self_:
                                values(g - 1)
                        if cross:
                            pe.wait_ge(sx_max, 4 * c + 4)
                            for h in range(4):
                                last = mm(PJ[1][:, h * T:(h + 1) * T], xrow_max[:, h, :], ident_r[0:T, 0:T], start=True, stop=True)
                            last.then_inc(mxt_done, 1)
                        if self_:
                            values(HKV - 1)
                        if more:
                            pe.wait_ge(x_split, b + 2)
                        if cross:
                            pe.wait_ge(mxt_read, c + 1)
                        def cross_scores_t(n):
                            bank = PU[n % 2][0:T, 0:XC * T].rearrange("k (s q) -> k s q", s=4)
                            mm(bank, ident_r[0:T, 0:T], causal_t[:].unsqueeze(1).to_broadcast([T, XC, T]), start=True, stop=False)
                            bank = PU[n % 2][0:T, 0:XC * T]
                            mm(bank, select[:, HKV + n:HKV + n + 1].to_broadcast([P, T]), xmaxT[:], start=False, stop=False)
                            three_passes(bank, xkT_hi[:, n, :], xkT_lo[:, n, :], xqT_hi[:, n], xqT_lo[:, n], False, True)\
                                .then_inc(stx_done, 1)

                        def cross_values(n):
                            pe.wait_ge(expx_done, 4 * c + n + 1)
                            for i in range(4):
                                last = mm(PT[n // 2][64 * (n % 2):64 * (n % 2) + 64, i * T:(i + 1) * T],
                                          xv_wide[:, XC * i + n, :], probs[:, n, i, :], start=True, stop=True)
                            last.then_inc(pvx_done, 1)

                        if cross:
                            cross_scores_t(0)
                        if more:
                            for k in range(KC):
                                project_qkv(k)
                        if cross:
                            if outp:
                                pe.wait_ge(yres_added, y + 1)
                            cross_values(0)
                            cross_scores_t(1)
                        if self_:
                            if isinstance(it, int) and it == 0:
                                pe.wait_ge(w_ready, w_order["o"] + 1)
                            pe.wait_ge(ot_split, b + 1)
                            for k in range(KC // 2):
                                project_chunk(PO[1][0:T, :], oT_hi, oT_lo, "o", k)
                        if cross:
                            cross_values(1)
                            cross_scores_t(2)
                        if self_:
                            for k in range(KC // 2, KC):
                                last = project_chunk(PO[1][0:T, :], oT_hi, oT_lo, "o", k)
                            last.then_inc(wo_done, 1)
                        if more:
                            transpose_k(b + 1)
                        if cross:
                            cross_scores_t(3)
                            cross_values(2)
                            cross_values(3)
                    pipeline(pe, step)

        x2T = sb("x2T", [P, NG, GB, KC, T])
        ew_hi = [sb(f"ew_hi{e}", [P, KC, D], F32R) for e in range(E)]
        xg_hi = [sb(f"xg_hi{i}", [P, KC, GB, T], F32R) for i in range(2)]
        with ExitStack() as same_place:
            ew_in = [sb(f"ew_in{e}", [P, KC, D], F32, same_place) for e in range(E)]
            xg_in = [sb("xg_in0", [P, KC, GB, T], F32, same_place), xg_in1]
        ew_lo = [sb(f"ew_lo{e}", [P, KC, D], F32R) for e in range(E)]
        xg_lo = [sb("xg_lo0", [P, KC, GB, T], F32R), xg_lo1]
        gate_in = sb("gate_in", [P, KC, E])
        ids = sb("ids", [T, E])
        logits = sb("logits", [T, B, E])
        top = sb("top", [T, B, 8])
        top_at = sb("top_at", [T, B, 8], U32)
        top_atf = sb("top_atf", [T, B, 2])
        diff = sb("diff", [T, B])
        ex = sb("ex", [T, B])
        denom = sb("denom", [T, B])
        share = sb("share", [T, 2, B])
        gates = sb("gates", [T, B, E])
        fstats = sb("fstats", [T, GB, 6])
        fmoments = sb("fmoments", [T, GB, 2])
        fvar = sb("fvar", [T, GB])
        frstd = sb("frstd", [T, GB])

        def last_group(tg):
            return isinstance(tg, int) and tg == NG - 1

        def back_bank(tg):
            return PT + PJ if last_group(tg) else PT + PT

        def groups(eng, group):
            group(0)
            with eng.Fori(1, NG) as tg:
                group(tg)

        with nc.Block() as block:

            @block.sync
            def _(sp):
                def load_expert(e):
                    sp.dma_start(ew_in[e][:], w_exp.rearrange("e (c p) n -> e p c n", p=P)[e])\
                      .then_inc(ew_loaded[e], 16)

                sp.dma_start(gate_in[:], w_gate.rearrange("(c p) e -> p c e", p=P)).then_inc(gate_loaded, 16)
                load_expert(0)
                sp.dma_start(ids[:], expert_ids_c).then_inc(ids_loaded, 16)
                for e in range(1, E):
                    load_expert(e)
                sp.wait_ge(t2_done, B)
                sp.dma_start(eb_in, b_exp).then_inc(eb_loaded, 16)
                with sp.Fori(0, NG) as tg:
                    for i in range(GB):
                        sp.wait_ge(fin_ready, tg * GB + i + 1)
                        sp.dma_start(out[tg * GB + i], fin[:, i, :]).then_inc(fin_free[i], 16)
                for i in range(GB):
                    sp.wait_ge(fin_free[i], 16 * (NG + 1))

            @block.scalar
            def _(act):
                def copy(dst, src):
                    return nc.scalar.activation(dst, src, ACT.Copy)

                def high_expert(e):
                    act.wait_ge(ew_loaded[e], 16)
                    copy(ew_hi[e][:], ew_in[e][:]).then_inc(ew_high, 1)

                def logits_copy(g):
                    act.wait_ge(gate_done, g + 1)
                    copy(logits[:, g * GB:(g + 1) * GB], PT[0][0:T, 0:GB * E].rearrange("t (b e) -> t b e", b=GB))\
                        .then_inc(logits_ready, 1)

                def top_exps(g):
                    act.wait_ge(diff_done, g + 1)
                    nc.scalar.activation(ex[:, g * GB:(g + 1) * GB], diff[:, g * GB:(g + 1) * GB], ACT.Exp).then_inc(top_exp, 1)

                def gates_copy(g):
                    act.wait_ge(gt_done, g + 1)
                    copy(gT_hi[:, g], PT[1][0:E, 0:GT]).then_inc(gt_high, 1)

                for b in range(0, B, 2):
                    act.wait_ge(t2_done, b + 1)
                    copy(x2T[:, b // GB, b % GB], TB[b % 4][:, 0:KC * T]).then_inc(t2_even, 1)
                    if b == GB:
                        high_expert(0)
                        logits_copy(0)
                    if b == GB + 2:
                        top_exps(0)
                act.wait_ge(moe_zeroed, 1)
                gates_copy(0)
                high_expert(1)

                def group(tg):
                    for e in range(E):
                        act.wait_ge(scaled, tg * E + e + 1)
                        copy(xg_hi[e % 2][:], xg_in[e % 2][:]).then_inc(xg_high, 1)
                        if isinstance(tg, int):
                            if e % 2 == 0 and 0 < e // 2 < NG:
                                logits_copy(e // 2)
                                top_exps(e // 2)
                            if e % 2 == 1 and 0 < e // 2 < NG:
                                gates_copy(e // 2)
                            if e + 2 < E:
                                high_expert(e + 2)
                            if e == 4:
                                act.wait_ge(moe_zeroed, 3)
                                act.wait_ge(eb_loaded, 16)
                                copy(eb_hi[0:E], eb_in).then_inc(eb_high, 1)
                                copy(eb_hi[LO:LO + E], eb_in).then_inc(eb_high, 1)
                groups(act, group)

            @block.gpsimd
            def _(pool):
                def low_expert(e):
                    pool.wait_ge(ew_high, e + 1)
                    nc.gpsimd.tensor_tensor(ew_lo[e][:], ew_in[e][:], ew_hi[e][:].bitcast(F32), ALU.subtract)\
                        .then_inc(ew_split, 1)

                pool.wait_ge(t2_done, GB)
                nc.gpsimd.memset(gT[:].bitcast(F32), 0.0).then_inc(moe_zeroed, 1)
                nc.gpsimd.tensor_tensor(spread[:], ident[:, 0:E], ident[:, LO:LO + E], ALU.add).then_inc(eb_split, 1)
                low_expert(0)
                pool.wait_ge(t2_done, B)
                nc.gpsimd.memset(eb_hi[:].bitcast(F32), 0.0).then_inc(moe_zeroed, 1)
                nc.gpsimd.memset(eb_lo[:].bitcast(F32), 0.0).then_inc(moe_zeroed, 1)
                for i in range(GB):
                    nc.gpsimd.memset(fin[:, i, 0:1], 0.0).then_inc(fin_free[i], 16)
                for e in range(1, E):
                    low_expert(e)
                pool.wait_ge(moe_zeroed, 3)
                pool.wait_ge(eb_high, 2)
                nc.gpsimd.tensor_tensor(eb_lo[0:E], eb_in, eb_hi[0:E].bitcast(F32), ALU.subtract).then_inc(eb_split, 1)
                with pool.Fori(0, NG) as tg:
                    for i in range(GB):
                        pool.wait_ge(fin_mom, tg * GB + i + 1)
                        nc.gpsimd.tensor_tensor(fvar[:, i:i + 1], fmoments[:, i, 1:2], eps_col[:], ALU.add)\
                            .then_inc(fin_eps, 1)
                        pool.wait_ge(fin_eps, tg * GB + i + 1)
                        nc.gpsimd.tensor_tensor(frstd[:, i:i + 1], fvar[:, i:i + 1], minus_half[:], ALU.pow)\
                            .then_inc(fin_rstd, 1)

            @block.vector
            def _(dve):
                v = nc.vector
                def route(g):
                    at = slice(g * GB, (g + 1) * GB)
                    dve.wait_ge(logits_ready, g + 1)
                    for b in range(g * GB, (g + 1) * GB):
                        v.max(top[:, b, :], logits[:, b, :]).then_inc(top_ready, 1)
                    for b in range(g * GB, (g + 1) * GB):
                        dve.wait_ge(top_ready, b + 1)
                        v.max_index(top_at[:, b, :], top[:, b, :], logits[:, b, :]).then_inc(top_index, 1)
                    v.tensor_tensor(diff[:, at], top[:, at, 1], top[:, at, 0], ALU.subtract).then_inc(diff_done, 1)
                    dve.wait_ge(top_index, (g + 1) * GB)
                    v.tensor_copy(top_atf[:, at], top_at[:, at, 0:2]).then_inc(top_step, 1)
                    dve.wait_ge(ids_loaded, 16)
                    dve.wait_ge(top_step, 8 * g + 1)
                    for r in range(2):
                        v.tensor_tensor(pick[:, r, at], ids[:].unsqueeze(1).to_broadcast([T, GB, E]),
                                        top_atf[:, at, r].unsqueeze(2).to_broadcast([T, GB, E]), ALU.is_equal)\
                            .then_inc(top_step, 1)
                    dve.wait_ge(top_exp, g + 1)
                    v.tensor_scalar(denom[:, at], ex[:, at], 1.0, None, ALU.add).then_inc(top_step, 1)
                    dve.wait_ge(top_step, 8 * g + 4)
                    v.reciprocal(share[:, 0, at], denom[:, at]).then_inc(top_step, 1)
                    dve.wait_ge(top_step, 8 * g + 5)
                    v.tensor_tensor(share[:, 1, at], ex[:, at], share[:, 0, at], ALU.mult).then_inc(top_step, 1)
                    dve.wait_ge(top_step, 8 * g + 6)
                    for r in range(2):
                        v.tensor_tensor(pick[:, r, at], pick[:, r, at], share[:, r, at].unsqueeze(2).to_broadcast([T, GB, E]),
                                        ALU.mult).then_inc(top_step, 1)
                    dve.wait_ge(top_step, 8 * g + 8)
                    v.tensor_tensor(gates[:, at], pick[:, 0, at], pick[:, 1, at], ALU.add).then_inc(gates_ready, 1)

                def low_gates(g):
                    dve.wait_ge(gt_high, g + 1)
                    v.tensor_tensor(gT_lo[:, g], PT[1][0:E, 0:GT], gT_hi[:, g].bitcast(F32), ALU.subtract)\
                        .then_inc(gt_split, 1)

                for b in range(1, B, 2):
                    dve.wait_ge(t2_done, b + 1)
                    v.tensor_copy(x2T[:, b // GB, b % GB], TB[b % 4][:, 0:KC * T].rearrange("p (c t) -> p c t", c=KC))\
                        .then_inc(t2_odd, 1)
                    if b == GB + 1:
                        route(0)
                low_gates(0)

                def scale(tg, e, fill=False):
                    n, s = tg * E + e, e % 2
                    dve.wait_ge(gb_done, n + 1)
                    if not fill:
                        dve.wait_ge(xg_used, n - 1)
                    v.tensor_tensor(xg_in[s][:], x2T[:, tg].rearrange("p b c t -> p c b t"),
                                    PJ[s][:, 0:GT].rearrange("p (b t) -> p b t", b=GB).unsqueeze(1)
                                    .to_broadcast([P, KC, GB, T]), ALU.mult).then_inc(scaled, 1)
                    dve.wait_ge(xg_high, n + 1)
                    v.tensor_tensor(xg_lo[s][:], xg_in[s][:], xg_hi[s][:].bitcast(F32), ALU.subtract)\
                        .then_inc(xg_split, 1)

                def add_residual(tg):
                    for oc in range(KC):
                        if oc < KC - 1:
                            dve.wait_ge(y_done, tg * (KC - 1) + oc + 1)
                        else:
                            dve.wait_ge(xg_used, tg * E + E)
                        v.tensor_tensor(sumT[:, oc].rearrange("p (b t) -> p b t", b=GB),
                                        PY[oc][:, 0:GT].rearrange("p (b t) -> p b t", b=GB), x2T[:, tg, :, oc, :], ALU.add)\
                            .then_inc(summed_t, 1)

                def normalise(tg, pair):
                    bank = back_bank(tg)
                    for i in (2 * pair, 2 * pair + 1):
                        dve.wait_ge(yt_done, tg * GB + i + 1)
                        v.bn_stats(fstats[:, i, :], bank[i][0:T, :]).then_inc(fin_stats, 1)
                        dve.wait_ge(const_ready, 12)
                        dve.wait_ge(fin_stats, tg * GB + i + 1)
                        v.bn_aggr(fmoments[:, i, :], fstats[:, i, :]).then_inc(fin_mom, 1)
                    for i in (2 * pair, 2 * pair + 1):
                        dve.wait_ge(fin_rstd, tg * GB + i + 1)
                        dve.wait_ge(fin_free[i], 16 * (tg + 1))
                        v.tensor_scalar(fin[:, i, :], bank[i][0:T, :], fmoments[:, i, 0:1], frstd[:, i:i + 1],
                                        ALU.subtract, ALU.mult).then_inc(fin_ready, 1)

                scale(0, 0, fill=True)
                scale(0, 1, fill=True)
                for e in range(2, E):
                    scale(0, e)
                    if e % 2 == 0 and e // 2 < NG:
                        route(e // 2)
                    if e % 2 == 1 and e // 2 < NG:
                        low_gates(e // 2)
                with dve.Fori(1, NG) as tg:
                    scale(tg, 0)
                    add_residual(tg - 1)
                    for e in range(1, E):
                        scale(tg, e)
                        if e == 2:
                            normalise(tg - 1, 0)
                        if e == 5:
                            normalise(tg - 1, 1)
                add_residual(NG - 1)
                normalise(NG - 1, 0)
                normalise(NG - 1, 1)

            @block.tensor
            def _(pe):
                mm = nc.tensor.matmul
                def gate_logits(g):
                    for b in range(g * GB, (g + 1) * GB):
                        for k in range(KC):
                            last = mm(PT[0][0:T, (b % GB) * E:(b % GB) * E + E], x2T[:, g, b % GB, k, :], gate_in[:, k, :],
                                      start=k == 0, stop=k == KC - 1)
                    last.then_inc(gate_done, 1)

                def transpose_gates(g):
                    pe.wait_ge(gates_ready, g + 1)
                    for i in range(GB):
                        last = nc.tensor.transpose(PT[1][0:E, i * T:(i + 1) * T], gates[:, g * GB + i, :], ident[0:T, 0:T])
                    last.then_inc(gt_done, 1)

                for b in range(B):
                    if b >= 4:
                        if b % 2 == 0:
                            pe.wait_ge(t2_even, (b - 4) // 2 + 1)
                        else:
                            pe.wait_ge(t2_odd, (b - 4) // 2 + 1)
                    if b == GB + 2:
                        pe.wait_ge(gate_loaded, 16)
                        pe.wait_ge(t2_odd, GB // 2)
                        gate_logits(0)
                    for k in range(KC):
                        last = nc.tensor.transpose(TB[b % 4][:, k * T:(k + 1) * T], x2[:, b, k * P:(k + 1) * P], ident[0:T, 0:T])
                    last.then_inc(t2_done, 1)
                transpose_gates(0)
                pe.wait_ge(t2_even, B // 2)
                pe.wait_ge(t2_odd, B // 2)
                pe.wait_ge(eb_split, 1)

                def spread_gates(tg, e, fill=False):
                    if not fill:
                        pe.wait_ge(scaled, tg * E + e - 1)
                    mm(PJ[e % 2][:, 0:GT], spread[:, e:e + 1].to_broadcast([P, P]), gT[:, tg], start=True, stop=True)\
                        .then_inc(gb_done, 1)

                def expert(tg, e):
                    pe.wait_ge(xg_split, tg * E + e + 1)
                    first = isinstance(tg, int) and tg == 0
                    if first:
                        pe.wait_ge(ew_split, e + 1)
                    for oc in range(KC):
                        cols, acc = slice(oc * P, (oc + 1) * P), PY[oc][:, 0:GT]
                        if e == 0 and not first:
                            pe.wait_ge(summed_t, (tg - 1) * KC + oc + 1)
                        if e == E - 1:
                            if first and oc == 0:
                                pe.wait_ge(eb_split, 2)
                            mm(acc, eb_hi[:, cols], gT[:, tg], start=False, stop=False)
                            mm(acc, eb_lo[:, cols], gT[:, tg], start=False, stop=False)
                        for k in range(KC):
                            last = three_passes(acc, ew_hi[e][:, k, cols], ew_lo[e][:, k, cols], xg_hi[e % 2][:, k], xg_lo[e % 2][:, k],
                                                e == 0 and k == 0, e == E - 1 and k == KC - 1)
                        if oc == KC - 1:
                            last.then_inc(xg_used, 1)
                        elif e == E - 1:
                            last.then_inc(y_done, 1)

                def back(tg, pair):
                    for i in (2 * pair, 2 * pair + 1):
                        if pair == 0 or last_group(tg):
                            pe.wait_ge(summed_t, tg * KC + KC)
                        else:
                            pe.wait_ge(fin_ready, tg * GB + i - 1)
                        for k in range(KC):
                            last = nc.tensor.transpose(back_bank(tg)[i][0:T, k * P:(k + 1) * P], sumT[:, k, i * T:(i + 1) * T], ident[:])
                        last.then_inc(yt_done, 1)

                pe.wait_ge(gt_split, 1)
                spread_gates(0, 0, fill=True)
                for e in range(E):
                    if e + 1 < E:
                        spread_gates(0, e + 1, fill=e == 0)
                    else:
                        spread_gates(1, 0)
                    expert(0, e)
                    if e % 2 == 0 and 0 < e // 2 < NG:
                        transpose_gates(e // 2)
                    if e % 2 == 0 and e // 2 + 1 < NG:
                        gate_logits(e // 2 + 1)
                pe.wait_ge(gt_split, NG)
                with pe.Fori(1, NG - 1) as tg:
                    for e in range(E):
                        if e + 1 < E:
                            spread_gates(tg, e + 1)
                        else:
                            spread_gates(tg + 1, 0)
                        expert(tg, e)
                        if e == 0:
                            back(tg - 1, 0)
                        if e == 3:
                            back(tg - 1, 1)
                for e in range(E):
                    if e + 1 < E:
                        spread_gates(NG - 1, e + 1)
                    expert(NG - 1, e)
                    if e == 0:
                        back(NG - 2, 0)
                    if e == 3:
                        back(NG - 2, 1)
                back(NG - 1, 0)
                back(NG - 1, 1)


def kernel(x, ctx_512, L0_attn_Wq, L0_attn_bq, L0_attn_Wk, L0_attn_bk, L0_attn_Wv, L0_attn_bv, L0_attn_Wo, L0_attn_bo,
           L0_xattn_Wq, L0_xattn_Wkv_expand, L0_xattn_Wout, L0_ffn_gate_w, L0_ffn_expert_w, L0_ffn_expert_b):
    import numpy as np
    import concourse.bacc as bacc
    from concourse.bass_utils import run_bass_kernel_spmd

    def q_order(w):
        return w.reshape(2, 4, J, HD, -1).transpose(0, 2, 1, 3, 4).reshape(D, -1)

    def x_order(w):
        return w.reshape(4, XC, XD, -1).transpose(1, 0, 2, 3).reshape(D, -1)

    def rows(v):
        return np.broadcast_to(np.asarray(v)[None, :], (T, v.shape[0]))

    x, ctx = np.asarray(x), np.asarray(ctx_512)
    wq, bq = q_order(np.asarray(L0_attn_Wq)), q_order(np.asarray(L0_attn_bq)[:, None])[:, 0]
    wkv = np.asarray(L0_xattn_Wkv_expand)
    inv_freq = (1.0 / 10000.0 ** (np.arange(0, HD, 2, dtype=np.float32) / HD)).astype(np.float32)
    ang = np.arange(T, dtype=np.float32)[:, None] * inv_freq[None, :]
    cos, sin = np.cos(ang), np.sin(ang)
    select = np.zeros((P, HKV + XC), np.float32)
    for g in range(HKV):
        select[32 * (g % 4) + g // 4, g] = -1.0
    for n in range(XC):
        select[32 * n + 2, HKV + n] = -1.0
    causal = np.where(np.arange(T)[None, :] <= np.arange(T)[:, None], 0.0, -1e30).astype(np.float32)
    arrays = {
        "x": x,
        "xT": x.reshape(B * T, D).T,
        "ctxT": ctx[:, :T, :].reshape(B * T, P).T,
        "w_qkv": np.concatenate([wq, np.asarray(L0_attn_Wk), np.asarray(L0_attn_Wv)]).T,
        "b_qkv": rows(np.concatenate([bq, np.asarray(L0_attn_bk), np.asarray(L0_attn_bv)])),
        "w_o": np.asarray(L0_attn_Wo).T.reshape(HKV, J, HD, D).transpose(1, 0, 2, 3).reshape(D, D),
        "b_o": rows(L0_attn_bo),
        "w_xkv": np.concatenate([x_order(wkv[:D]), wkv[D:]]).T,
        "w_xq": x_order(np.asarray(L0_xattn_Wq)).T,
        "w_xo": np.asarray(L0_xattn_Wout).T,
        "w_gate": np.asarray(L0_ffn_gate_w).T,
        "w_exp": np.asarray(L0_ffn_expert_w),
        "b_exp": np.asarray(L0_ffn_expert_b),
        "rope_cos": np.concatenate([cos, cos], 1),
        "rope_sin": np.concatenate([-sin, sin], 1),
        "ident": np.eye(P, dtype=np.float32),
        "select": select,
        "causal": causal,
        "causal_t": causal.T,
        "expert_ids": np.broadcast_to(np.arange(E, dtype=np.float32)[None, :], (T, E)),
    }
    arrays = {f"in_{k}": np.ascontiguousarray(v) for k, v in arrays.items()}
    nc = bacc.Bacc("TRN2", target_bir_lowering=False, num_devices=1)
    args = [nc.dram_tensor(k, v.shape, mybir.dt.from_np(v.dtype), kind="ExternalInput").ap() for k, v in arrays.items()]
    args.append(nc.dram_tensor("out", (B, T, D), F32, kind="ExternalOutput").ap())
    build_decoder(nc, *args)
    r = run_bass_kernel_spmd(nc, [arrays], core_ids=[0])
    return r.results[0]["out"]
```
